# Optimizing a Trainium2 kernel written in Bass

```python
import numpy as np
import jax
import jax.numpy as jnp

def _softmax(x, axis=-1):
    return jax.nn.softmax(x, axis=axis)

def _gelu(x):
    return jax.nn.gelu(x, approximate=True)

def _silu(x):
    return jax.nn.silu(x)

def _sigmoid(x):
    return jax.nn.sigmoid(x)

def _layernorm(x, axis=-1, eps=1e-05):
    m = jnp.mean(x, axis=axis, keepdims=True)
    v = jnp.var(x, axis=axis, keepdims=True)
    return (x - m) / jnp.sqrt(v + eps)

def _scatter_add(tgt, idx, src, axis=0):
    return tgt.at[idx].add(src)

def _segment_sum(src, seg, n):
    return jax.ops.segment_sum(src, seg, n)
kernel_name = 'mk_sandwich_d1_jaxref_r4_25b3a3'

def setup_inputs(seed: int=0):
    np.random.seed(seed)
    _w = jnp.asarray

    def _L0_attn_setup():
        import jax, jax.numpy as jnp
        import numpy as np
        D_MODEL = 256
        N_HEADS = 16
        LOCAL_W = 128
        GLOBAL_W = 256
        LN_EPS = 1e-05

        def _mha(x, W_in, b_in, W_out, b_out, mask):
            B, T, D = x.shape
            hd = D // N_HEADS
            qkv = x @ W_in.T + b_in
            q, k, v = jnp.split(qkv, 3, axis=-1)

            def heads(t):
                return t.reshape(B, T, N_HEADS, hd).transpose(0, 2, 1, 3)
            q, k, v = (heads(q), heads(k), heads(v))
            scale = 1.0 / jnp.sqrt(jnp.asarray(hd, x.dtype))
            scores = jnp.einsum('bhqd,bhkd->bhqk', q, k) * scale + mask
            a = jax.nn.softmax(scores, axis=-1)
            o = jnp.einsum('bhqk,bhkd->bhqd', a, v).transpose(0, 2, 1, 3).reshape(B, T, D)
            return o @ W_out.T + b_out

        def _sliding_window_attn(q, W_in, b_in, W_out, b_out, window):
            B, S, D = q.shape
            nw = (S + window - 1) // window
            pad = nw * window - S
            if pad > 0:
                q = jnp.pad(q, ((0, 0), (0, pad), (0, 0)))
            qw = q.reshape(B * nw, window, D)
            mask = jnp.triu(jnp.ones((window, window), dtype=q.dtype), k=1)
            out = _mha(qw, W_in, b_in, W_out, b_out, mask)
            return out.reshape(B, nw * window, D)[:, :S, :]
        key = jax.random.key(seed)
        ks = jax.random.split(key, 12)
        D = D_MODEL
        s = 1.0 / np.sqrt(D)
        pl, _ = jnp.linalg.qr(jax.random.normal(ks[0], (D, D), jnp.float32))
        pg, _ = jnp.linalg.qr(jax.random.normal(ks[1], (D, D), jnp.float32))
        return {'x': jax.random.normal(ks[2], (2, 1024, D), jnp.float32), 'proj_local': pl, 'proj_global': pg, 'Wl_in': jax.random.uniform(ks[3], (3 * D, D), jnp.float32, -s, s), 'bl_in': jnp.zeros((3 * D,), jnp.float32), 'Wl_out': jax.random.uniform(ks[4], (D, D), jnp.float32, -s, s), 'bl_out': jnp.zeros((D,), jnp.float32), 'Wg_in': jax.random.uniform(ks[5], (3 * D, D), jnp.float32, -s, s), 'bg_in': jnp.zeros((3 * D,), jnp.float32), 'Wg_out': jax.random.uniform(ks[6], (D, D), jnp.float32, -s, s), 'bg_out': jnp.zeros((D,), jnp.float32), 'fusion_w': jnp.ones((2,), jnp.float32), 'ln_gamma': jnp.ones((D,), jnp.float32), 'ln_beta': jnp.zeros((D,), jnp.float32)}
    _L0_attn_in = _L0_attn_setup()

    def _L0_ffn_setup():
        import math
        import jax, jax.numpy as jnp
        import numpy as np
        CAPACITY_FACTOR = 1.25
        key = jax.random.key(seed)
        ks = jax.random.split(key, 5)
        B, S, H, F, E = (4, 1024, 256, 256, 32)
        scale_in = 1.0 / math.sqrt(H)
        scale_mid = 1.0 / math.sqrt(F)
        return {'x': jax.random.normal(ks[0], (B, S, H), dtype=jnp.float32), 'w_router': jax.random.normal(ks[1], (H, E), dtype=jnp.float32) * scale_in, 'w_gate': jax.random.normal(ks[2], (E, H, F), dtype=jnp.float32) * scale_in, 'w_up': jax.random.normal(ks[3], (E, H, F), dtype=jnp.float32) * scale_in, 'w_down': jax.random.normal(ks[4], (E, F, H), dtype=jnp.float32) * scale_mid}
    _L0_ffn_in = _L0_ffn_setup()
    _d = {'L0_attn_x': _L0_attn_in['x'], 'L0_attn_proj_local': _L0_attn_in['proj_local'], 'L0_attn_proj_global': _L0_attn_in['proj_global'], 'L0_attn_Wl_in': _L0_attn_in['Wl_in'], 'L0_attn_bl_in': _L0_attn_in['bl_in'], 'L0_attn_Wl_out': _L0_attn_in['Wl_out'], 'L0_attn_bl_out': _L0_attn_in['bl_out'], 'L0_attn_Wg_in': _L0_attn_in['Wg_in'], 'L0_attn_bg_in': _L0_attn_in['bg_in'], 'L0_attn_Wg_out': _L0_attn_in['Wg_out'], 'L0_attn_bg_out': _L0_attn_in['bg_out'], 'L0_attn_fusion_w': _L0_attn_in['fusion_w'], 'L0_attn_ln_gamma': _L0_attn_in['ln_gamma'], 'L0_attn_ln_beta': _L0_attn_in['ln_beta'], 'L0_ffn_w_router': _L0_ffn_in['w_router'], 'L0_ffn_w_gate': _L0_ffn_in['w_gate'], 'L0_ffn_w_up': _L0_ffn_in['w_up'], 'L0_ffn_w_down': _L0_ffn_in['w_down']}
    _x0 = _d['L0_attn_x']
    _d['L0_attn_x'] = jax.random.normal(jax.random.fold_in(jax.random.key(seed), 1), (16, 512, 256), dtype=_x0.dtype)
    del _x0
    return _d

def reference(L0_attn_x, L0_attn_proj_local, L0_attn_proj_global, L0_attn_Wl_in, L0_attn_bl_in, L0_attn_Wl_out, L0_attn_bl_out, L0_attn_Wg_in, L0_attn_bg_in, L0_attn_Wg_out, L0_attn_bg_out, L0_attn_fusion_w, L0_attn_ln_gamma, L0_attn_ln_beta, L0_ffn_w_router, L0_ffn_w_gate, L0_ffn_w_up, L0_ffn_w_down):

    def _L0_attn_ref(x, proj_local, proj_global, Wl_in, bl_in, Wl_out, bl_out, Wg_in, bg_in, Wg_out, bg_out, fusion_w, ln_gamma, ln_beta):
        import jax, jax.numpy as jnp
        import numpy as np
        D_MODEL = 256
        N_HEADS = 16
        LOCAL_W = 128
        GLOBAL_W = 256
        LN_EPS = 1e-05

        def _mha(x, W_in, b_in, W_out, b_out, mask):
            B, T, D = x.shape
            hd = D // N_HEADS
            qkv = x @ W_in.T + b_in
            q, k, v = jnp.split(qkv, 3, axis=-1)

            def heads(t):
                return t.reshape(B, T, N_HEADS, hd).transpose(0, 2, 1, 3)
            q, k, v = (heads(q), heads(k), heads(v))
            scale = 1.0 / jnp.sqrt(jnp.asarray(hd, x.dtype))
            scores = jnp.einsum('bhqd,bhkd->bhqk', q, k) * scale + mask
            a = jax.nn.softmax(scores, axis=-1)
            o = jnp.einsum('bhqk,bhkd->bhqd', a, v).transpose(0, 2, 1, 3).reshape(B, T, D)
            return o @ W_out.T + b_out

        def _sliding_window_attn(q, W_in, b_in, W_out, b_out, window):
            B, S, D = q.shape
            nw = (S + window - 1) // window
            pad = nw * window - S
            if pad > 0:
                q = jnp.pad(q, ((0, 0), (0, pad), (0, 0)))
            qw = q.reshape(B * nw, window, D)
            mask = jnp.triu(jnp.ones((window, window), dtype=q.dtype), k=1)
            out = _mha(qw, W_in, b_in, W_out, b_out, mask)
            return out.reshape(B, nw * window, D)[:, :S, :]
        lqs = x @ proj_local
        gqs = x @ proj_global
        local_out = _sliding_window_attn(lqs, Wl_in, bl_in, Wl_out, bl_out, LOCAL_W)
        global_out = _sliding_window_attn(gqs, Wg_in, bg_in, Wg_out, bg_out, GLOBAL_W)
        w = jax.nn.softmax(fusion_w, axis=0)
        fused = w[0] * local_out + w[1] * global_out
        mu = jnp.mean(fused, axis=-1, keepdims=True)
        var = jnp.mean(jnp.square(fused - mu), axis=-1, keepdims=True)
        return (fused - mu) * jax.lax.rsqrt(var + LN_EPS) * ln_gamma + ln_beta

    def _L0_ffn_ref(x, w_router, w_gate, w_up, w_down):
        import math
        import jax, jax.numpy as jnp
        import numpy as np
        CAPACITY_FACTOR = 1.25
        B, S, H = x.shape
        E = w_gate.shape[0]
        T = B * S
        C = int(math.ceil(CAPACITY_FACTOR * T / E))
        xt = x.reshape(T, H)
        logits = xt @ w_router
        probs = jax.nn.softmax(logits, axis=-1)
        top1 = jnp.argmax(probs, axis=-1)
        gate = jnp.take_along_axis(probs, top1[:, None], axis=1)[:, 0]
        onehot = jax.nn.one_hot(top1, E, dtype=jnp.int32)
        pos = jnp.cumsum(onehot, axis=0)[jnp.arange(T), top1] - 1
        accepted = pos < C
        slot = jnp.where(accepted, top1 * C + pos, E * C)
        buf = jnp.zeros((E * C + 1, H), dtype=x.dtype).at[slot].set(xt)
        buf = buf[:E * C].reshape(E, C, H)
        g = jnp.einsum('ech,ehf->ecf', buf, w_gate)
        u = jnp.einsum('ech,ehf->ecf', buf, w_up)
        y = jnp.einsum('ecf,efh->ech', jax.nn.silu(g) * u, w_down)
        out_tok = y.reshape(E * C, H)[jnp.clip(slot, 0, E * C - 1)]
        out_tok = jnp.where(accepted[:, None], out_tok * gate[:, None], 0.0)
        return (xt + out_tok).reshape(B, S, H)
    x = L0_attn_x
    x = x + _layernorm(_L0_attn_ref(_layernorm(x, axis=-1), L0_attn_proj_local, L0_attn_proj_global, L0_attn_Wl_in, L0_attn_bl_in, L0_attn_Wl_out, L0_attn_bl_out, L0_attn_Wg_in, L0_attn_bg_in, L0_attn_Wg_out, L0_attn_bg_out, L0_attn_fusion_w, L0_attn_ln_gamma, L0_attn_ln_beta), axis=-1)
    x = x + _layernorm(_L0_ffn_ref(_layernorm(x, axis=-1), L0_ffn_w_router, L0_ffn_w_gate, L0_ffn_w_up, L0_ffn_w_down), axis=-1)
    return x

_drawn_inputs = setup_inputs


def setup_inputs(seed=0):
    import zlib

    import numpy as np

    out = dict(_drawn_inputs(seed))
    spreads = {'L0_attn_bl_in': (0.0, 0.1),
     'L0_attn_bl_out': (0.0, 0.1),
     'L0_attn_bg_in': (0.0, 0.1),
     'L0_attn_bg_out': (0.0, 0.1),
     'L0_attn_fusion_w': (1.0, 0.6),
     'L0_attn_ln_gamma': (1.0, 0.2),
     'L0_attn_ln_beta': (0.0, 0.1)}
    factors = {}
    for name, (base, spread) in spreads.items():
        noise = np.random.default_rng([zlib.crc32(name.encode()), seed]).standard_normal(out[name].shape)
        drawn = base * np.exp(spread * noise) if base else spread * noise
        out[name] = jnp.asarray(drawn.astype(out[name].dtype))
    for name, factor in factors.items():
        out[name] = (out[name] * factor).astype(out[name].dtype)
    return out
```

```python
import concourse.bass as bass
from concourse import mybir
from contextlib import ExitStack

E_PARTS_Q = (0, 0, 0, 1, 1, 2)
E_PARTS_K = (0, 1, 2, 0, 1, 0)


def attention_moe_program(nc, T, x, pT_l, pT_g, winT_l, winT_g, woT_l, woT_g, bqk_l, bqk_g, bv_l, bv_g,
                          bo_l, bo_g, fusion_w, gamma, beta, w_router, w_gate, w_up, w_down, out):
    f32, bf16, u32 = mybir.dt.float32, mybir.dt.bfloat16, mybir.dt.uint32
    ALU, ACT, AX = mybir.AluOpType, mybir.ActivationFunctionType, mybir.AxisListType

    P = 128
    D = 256
    NH, HD = 16, 16
    WIN = 256
    NW = T // WIN
    E = 32
    CAP = -(-5 * T // (4 * E))
    NSLOT = E * CAP
    EPS = 1e-5
    QSCALE = 0.25
    UNITS = 24
    LU = 8
    GROUPS = 8
    NPART = 6 * HD
    KROWS = NPART + 3
    CHUNKS = [(r, min(P, CAP - r)) for r in range(0, CAP, P)]
    NCH = len(CHUNKS)
    ZROW = 2048
    N_ZERO = 16 * (-(-(NSLOT // P * D) // ZROW))

    def nth(w, per, k=0):
        i, c = w
        n = c * per + k + 1
        return n if i is None else i * (2 * per) + n

    def back(w, n=1):
        return (w[0], w[1] - n)

    def exists(w):
        return w[0] is not None or 0 <= w[1] < NW

    def num(w):
        return w[1] if w[0] is None else w[0] * 2 + w[1]

    def wait(eng, sem, w, per=1, k=0):
        if exists(w):
            eng.wait_ge(sem, nth(w, per, k))

    x_w = x.rearrange("b s f -> (b s) f").rearrange("(w q p) f -> w p q f", q=2, p=P)
    out_w = out.rearrange("b s f -> (b s) f").rearrange("(w q p) f -> w p q f", q=2, p=P)
    x1_d = nc.dram_tensor("x1_scratch", [T, D], f32).ap()
    slots_d = nc.dram_tensor("slots_scratch", [NSLOT, D], f32).ap()
    y_d = nc.dram_tensor("y_scratch", [NSLOT, D], f32).ap()
    x1_w = x1_d.rearrange("(w q p) f -> w p q f", q=2, p=P)

    with ExitStack() as ctx:
        def sb(name, shape, dt=f32, on=ctx):
            return on.enter_context(nc.sbuf_tensor(name, shape, dt))

        def sem(name):
            return ctx.enter_context(nc.semaphore(name))

        ident = sb("ident", [P, P])
        identb = sb("identb", [P, P], bf16)
        mask_g = sb("mask_g", [P, 4, P], bf16)
        tri = mask_g[:, 0, :]
        earlier = sb("earlier", [P, P], bf16)
        onesb = sb("onesb", [P, P], bf16)
        iota_e = sb("iota_e", [P, E])
        mhalf = sb("mhalf", [P, 2])
        weff = sb("weff", [P, 2, 2, 3 * D])
        wo = sb("wo", [P, 4, D])
        bqk = sb("bqk", [P, 2, 4])
        bias_row = sb("bias_row", [P, D])
        gamma_row = sb("gamma_row", [P, D])
        beta_row = sb("beta_row", [P, D])
        wr = sb("wr", [P, 2, E])
        st_all = sb("st_all", [P, NW, 4])
        gate_all = sb("gate_all", [P, NW, 2])
        slot_all = sb("slot_all", [P, NW, 2], u32)
        v_pad = sb("v_pad", [P, 2, 2, 2, NH, 32])
        xw = sb("xw", [P, 2, 2, D])
        xr = sb("xr", [P, 2, 2, D])
        xn = sb("xn", [P, 2, D])
        xnT = sb("xnT", [P, 2, WIN])
        x32 = sb("x32", [P, 2, 512])
        rest = sb("rest", [P, 2, 512])
        parts = sb("parts", [P, 2, 3, 512], bf16)
        mx = sb("mx", [P, 2, 2, NH])
        mneg = sb("mneg", [P, 2, 2, NH])
        mparts = sb("mparts", [P, 2, 2, 3, NH], bf16)
        mT = sb("mT", [48, 2, WIN], bf16)
        OT = sb("OT", [P, 2, 4, WIN])
        rden = sb("rden", [P, 2, NH])
        On = sb("On", [P, 2, 2, D])
        OnT = sb("OnT", [P, 2, 2, WIN])
        fbuf = sb("fbuf", [P, 2, D])
        ybuf = sb("ybuf", [P, 2, D])
        x1 = sb("x1", [P, 2, D])
        xn2 = sb("xn2", [P, 2, D])
        xn2T = sb("xn2T", [P, 2, WIN])
        bst = sb("bst", [P, 4, 2, 6])
        mv = sb("mv", [P, 4, 2, 2])
        ve = sb("ve", [P, 4, 2])
        rstd = sb("rstd", [P, 4, 2])
        lg = sb("lg", [P, 2, E])
        top = sb("top", [P, 2, 8])
        top_i = sb("top_i", [P, 2, 8], u32)
        ntop = sb("ntop", [P, 2])
        idx_f = sb("idx_f", [P, 2])
        hot = sb("hot", [P, 2, E], bf16)
        egate = sb("egate", [P, 2, E])
        gsum = sb("gsum", [P, 2])
        base = sb("base", [P, E])
        pos = sb("pos", [P, 2, E])
        posh = sb("posh", [P, 2, E])
        pos1 = sb("pos1", [P, 2])
        okf = sb("okf", [P, 2])
        slotf = sb("slotf", [P, 2])
        far = sb("far", [P, 2])
        gate1 = sb("gate1", [P, 2])
        slot_u = sb("slot_u", [P, 2, 2], u32)
        with ExitStack() as prep:
            pT = sb("pT", [P, 2, 2, D], on=prep)
            winT = sb("winT", [P, 2, 2, 3 * D], on=prep)
            bv = sb("bv", [P, 4], on=prep)
            bvb = sb("bvb", [P, 4, P], on=prep)
            bo = sb("bo", [P, 2, D], on=prep)
            fus = sb("fus", [P, 2], on=prep)
            fus_e = sb("fus_e", [P, 2], on=prep)
            fus_m = sb("fus_m", [P, 2], on=prep)
            zeros = sb("zeros", [P, ZROW], on=prep)
        with ExitStack() as attn:
            pt = sb("pt", [P, 8, 512], on=attn)
            stack = sb("stack", [P, 2, 2, 2, 8, 2, WIN], bf16, on=attn)
        with ExitStack() as experts:
            ew = sb("ew", [P, 2, 3, 2, D], on=experts)
            erows = sb("erows", [P, 2, NCH, D], on=experts)
            eT = sb("eT", [P, 2, 2, CAP], on=experts)
            sg = sb("sg", [P, 2, CAP], on=experts)
            hT = sb("hT", [P, 2, 2, CAP], on=experts)
            ybf = sb("ybf", [P, 2, NCH, D], on=experts)
            xc = sb("xc", [P, 2, 2, D], on=experts)
            yg = sb("yg", [P, 2, 2, D], on=experts)
            xn2c = sb("xn2c", [P, 2, D], on=experts)
            zc = sb("zc", [P, 2, 2, D], on=experts)
            oc = sb("oc", [P, 2, 2, D], on=experts)
            bst_c = sb("bst_c", [P, 2, 6], on=experts)
            mv_c = sb("mv_c", [P, 2, 2, 2], on=experts)
            ve_c = sb("ve_c", [P, 2, 2], on=experts)
            sd_c = sb("sd_c", [P, 2, 2], on=experts)
            rs_c = sb("rs_c", [P, 2, 2], on=experts)
            slot_c = sb("slot_c", [P, 2, 2], u32, on=experts)

        banks = [ctx.enter_context(nc.psum_tensor(f"bank{n}", [P, 512], f32)) for n in range(8)]
        S1, S2, PV, PJ, TR = banks[0:2], banks[2:4], banks[4], banks[5:7], banks[7]

        w_in = sem("w_in")
        w_fold = sem("w_fold")
        w_fold_out = sem("w_fold_out")
        fus_sem = sem("fus_sem")
        fus_exp = sem("fus_exp")
        wo_ready = sem("wo_ready")
        bias_ps = sem("bias_ps")
        const_pool = sem("const_pool")
        const_dve = sem("const_dve")
        zeroed = sem("zeroed")
        x_in = [sem("x_in0"), sem("x_in1")]
        xr_in = [sem("xr_in0"), sem("xr_in1")]
        ln_var = [sem(f"ln_var{n}") for n in range(4)]
        ln_rstd = [sem(f"ln_rstd{n}") for n in range(4)]
        xn_ready = sem("xn_ready")
        xnT_full = sem("xnT_full")
        xnT_ready = sem("xnT_ready")
        pj_full = sem("pj_full")
        v_full = sem("v_full")
        x32_ready = sem("x32_ready")
        hi_ready = sem("hi_ready")
        rest_ready = sem("rest_ready")
        mid_ready = sem("mid_ready")
        lo_ready = sem("lo_ready")
        spread = [sem(f"spread{n}") for n in range(4)]
        v_ready = sem("v_ready")
        s1_full = sem("s1_full")
        s1_read = sem("s1_read")
        mparts_ready = [sem("mparts_l"), sem("mparts_g")]
        mT_full = [sem("mT_full_l"), sem("mT_full_g")]
        mT_ready = [sem("mT_ready_l"), sem("mT_ready_g")]
        m_in = [sem("m_in_l"), sem("m_in_g")]
        s2_full = sem("s2_full")
        p_ready = sem("p_ready")
        pv_full = sem("pv_full")
        ot_ready = sem("ot_ready")
        nrm_full = [sem("nrm_full_l"), sem("nrm_full_g")]
        on_ready = [sem("on_ready_l"), sem("on_ready_g")]
        onT_full = [sem("onT_full_l"), sem("onT_full_g")]
        onT_ready = [sem("onT_ready_l"), sem("onT_ready_g")]
        o_full = sem("o_full")
        f_ready = sem("f_ready")
        n1_ready = sem("n1_ready")
        y_ready = sem("y_ready")
        z_ready = sem("z_ready")
        x1_ready = sem("x1_ready")
        x1_out = sem("x1_out")
        xn2_ready = sem("xn2_ready")
        x2T_full = sem("x2T_full")
        x2T_ready = sem("x2T_ready")
        lg_full = sem("lg_full")
        lg_ready = sem("lg_ready")
        hot_ready = sem("hot_ready")
        gsum_ready = sem("gsum_ready")
        cs_full = sem("cs_full")
        cs_read = sem("cs_read")
        slot_ready = sem("slot_ready")
        scat = sem("scat")

        ew_in = [sem("ew_in0"), sem("ew_in1")]
        er_in = [sem("er_in0"), sem("er_in1")]
        eT_full = sem("eT_full")
        eT_ready = sem("eT_ready")
        gu_full = sem("gu_full")
        sg_ready = sem("sg_ready")
        h_ready = sem("h_ready")
        ye_full = sem("ye_full")
        ya_ready = sem("ya_ready")
        yb_ready = sem("yb_ready")
        ye_out = [sem("ye_out0"), sem("ye_out1")]
        c_in = [sem("c_in0"), sem("c_in1")]
        c_idx = sem("c_idx")
        g_in = [sem("g_in0"), sem("g_in1")]
        c_var = sem("c_var")
        c_std = sem("c_std")
        c_nrm = sem("c_nrm")
        c_sum = sem("c_sum")
        c_out = [sem("c_out0"), sem("c_out1")]

        TR_USES = [("n_g0", 2, on_ready[1], 2, 0), ("n_g1", 2, on_ready[1], 2, 1), ("oT_g", 2, onT_ready[1], 1, 0),
                   ("op", 2, f_ready, 1, 0), ("n_l0", 1, on_ready[0], 2, 0), ("n_l1", 1, on_ready[0], 2, 1),
                   ("oT_l", 1, onT_ready[0], 1, 0), ("mT_l", 0, mT_ready[0], 1, 0), ("x2T", 2, x2T_ready, 1, 0),
                   ("lg", 2, lg_ready, 1, 0), ("cs", 2, cs_read, 1, 0), ("mT_g", 0, mT_ready[1], 1, 0)]
        PJ_USES = [("xnT", 0, xnT_ready, 1, 0), ("p0", 0, x32_ready, 4, 0), ("p1", 0, x32_ready, 4, 1),
                   ("v0", 0, v_ready, 2, 0), ("p2", 0, x32_ready, 4, 2), ("p3", 0, x32_ready, 4, 3),
                   ("v1", 0, v_ready, 2, 1)]

        def wait_alone(eng, sem, value):
            if not isinstance(value, int):
                value = eng.to_reg(value)
            eng.wait_ge(const_pool, 1)
            eng.wait_ge(sem, value)

        def wait_read(eng, uses, name, s, ago):
            at = [u[0] for u in uses].index(name)
            step, left = s, ago
            while left:
                at -= 1
                if at < 0:
                    at, step = len(uses) - 1, back(step)
                    if step[0] is None and step[1] < 0:
                        return
                w = back(step, uses[at][1])
                left -= exists(w)
            eng.wait_ge(uses[at][2], nth(w, uses[at][3], uses[at][4]))

        def pj_bank(name, par):
            return PJ[([u[0] for u in PJ_USES].index(name) + par) % 2]

        def steps(eng, one):
            for s in range(4):
                one((None, s), s % 2)
            with eng.Fori(0, (NW - 6) // 2) as i:
                one((i, 4), 0)
                one((i, 5), 1)
            for s in range(NW - 2, NW + 2):
                one((None, s), s % 2)

        def each_expert(eng, one):
            for e in range(2):
                one((None, e), e)
            with eng.Fori(0, (E - 4) // 2) as i:
                one((i, 2), 0)
                one((i, 3), 1)
            for e in range(E - 2, E):
                one((None, e), e % 2)

        def alternate(w, per):
            i, n = w
            n = per * (n // 2 + 1)
            return n if i is None else i * per + n

        def ebefore(e, n=1):
            e = back(e, n)
            return e if e[0] is not None or e[1] >= 0 else None

        def stages(s):
            return [w if exists(w) else None for w in (s, back(s, 1), back(s, 2))]

        def q_stack(par, b, h, lo, n, rows=KROWS):
            return stack[0:rows, par, b, 0, h % 8, h // 8, lo:lo + n]

        def k_stack(par, b, h, lo, n, rows=KROWS):
            return stack[0:rows, par, b, 1, h % 8, h // 8, lo:lo + n]

        block = ctx.enter_context(nc.Block())

        @block.sync
        def _(sp):
            for b, (p_, w_, o_, k_, v_, c_) in enumerate(((pT_l, winT_l, woT_l, bqk_l, bv_l, bo_l),
                                                          (pT_g, winT_g, woT_g, bqk_g, bv_g, bo_g))):
                sp.dma_start(pT[:, b, :, :], p_.rearrange("(c p) n -> p c n", p=P)).then_inc(w_in, 16)
                sp.dma_start(winT[:, b, :, :], w_.rearrange("(c p) n -> p c n", p=P)).then_inc(w_in, 16)
                sp.dma_start(wo[:, 2 * b:2 * b + 2, :], o_.rearrange("(c p) n -> p c n", p=P)).then_inc(w_in, 16)
                sp.dma_start(bqk[:, b, :], k_).then_inc(w_in, 16)
                sp.dma_start(bv[:, 2 * b:2 * b + 2], v_).then_inc(w_in, 16)
                sp.dma_start(bo[:, b, :], c_.partition_broadcast(P)).then_inc(w_in, 16)
            sp.dma_start(fus[:, :], fusion_w.partition_broadcast(P)).then_inc(w_in, 16)
            sp.dma_start(gamma_row[:, :], gamma.partition_broadcast(P)).then_inc(w_in, 16)
            sp.dma_start(beta_row[:, :], beta.partition_broadcast(P)).then_inc(w_in, 16)
            sp.dma_start(wr[:, :, :], w_router.rearrange("(c p) n -> p c n", p=P)).then_inc(w_in, 16)
            sp.dma_start(xw[:, 0, :, :], x_w[0]).then_inc(x_in[0], 16)
            sp.wait_ge(const_dve, 1)
            flat = slots_d.rearrange("(p r) f -> p (r f)", p=P)
            n_flat = NSLOT // P * D
            for lo in range(0, n_flat, ZROW):
                n = min(ZROW, n_flat - lo)
                sp.dma_start(flat[:, lo:lo + n], zeros[:, 0:n]).then_inc(zeroed, 16)
            sp.wait_ge(zeroed, N_ZERO)
            sp.wait_ge(w_fold, 8)

            def step(s, par):
                a, c, d = stages(s)
                nxt = back(s, -1)
                dyn_a = num(nxt) if a and (nxt[0] is not None or nxt[1] < NW) else None
                dyn_d = num(d) if d else None
                if a and dyn_a is not None:
                    if exists(back(a)):
                        wait_alone(sp, xn_ready, nth(back(a), 1))
                    sp.dma_start(xw[:, 1 - par, :, :], x_w[bass.ds(dyn_a, 1)].rearrange("w p q f -> (w p) q f")
                                 ).then_inc(x_in[1 - par], 16)
                if d:
                    if exists(back(d, 2)):
                        wait_alone(sp, x1_ready, nth(back(d, 2), 1))
                    sp.dma_start(xr[:, par, :, :], x_w[bass.ds(dyn_d, 1)].rearrange("w p q f -> (w p) q f")
                                 ).then_inc(xr_in[par], 16)
                if a:
                    if exists(back(a, 2)):
                        wait_alone(sp, s2_full, nth(back(a, 2), UNITS, UNITS - 1))
                    for j in range(4):
                        b, qk = j // 2, j % 2
                        wait_alone(sp, lo_ready, nth(a, 4, j))
                        for n, part in enumerate((E_PARTS_Q, E_PARTS_K)[qk]):
                            sp.dma_start(stack[HD * n:HD * n + HD, par, b, qk, :, :, :].rearrange("d h t n -> d h (t n)"),
                                         parts[:, j % 2, part, :]).then_inc(spread[j], 16)
                if d:
                    wait_alone(sp, x1_ready, nth(d, 1))
                    sp.dma_start(x1_w[bass.ds(dyn_d, 1)].rearrange("w p q f -> (w p) q f"), x1[:, :, :]).then_inc(x1_out, 16)
                if a:
                    for b in range(2):
                        wait_alone(sp, mT_ready[b], nth(a, 1))
                        sp.dma_start(stack[NPART:KROWS, par, b, 0, :, :, :].rearrange("r h t n -> r (h t) n"),
                                     mT[:, b, :]).then_inc(m_in[b], 16)

            steps(sp, step)

            sp.wait_ge(pv_full, GROUPS * NW)
            sp.wait_ge(scat, 32 * NW)
            w_e = [w.rearrange("e (c p) f -> e p c f", p=P) for w in (w_gate, w_up, w_down)]
            rows_e = slots_d.rearrange("(e r) f -> e r f", e=E)
            y_e = y_d.rearrange("(e r) f -> e r f", e=E)

            def store(e, par, number):
                for n, (r, m) in enumerate(CHUNKS):
                    sp.dma_start(y_e[bass.ds(number, 1), r:r + m, :].rearrange("e r f -> (e r) f"), ybf[0:m, par, n, :]
                                 ).then_inc(ye_out[par], 16)

            def expert(e, par):
                prev = ebefore(e, 2)
                number, old = num(e), num(prev) if prev else None
                if prev:
                    wait_alone(sp, eT_full, nth(prev, 1))
                for n, (r, m) in enumerate(CHUNKS):
                    sp.dma_start(erows[0:m, par, n, :], rows_e[bass.ds(number, 1), r:r + m, :].rearrange("e r f -> (e r) f")
                                 ).then_inc(er_in[par], 16)
                if prev:
                    wait_alone(sp, ye_full, nth(prev, 1))
                for n in range(3):
                    sp.dma_start(ew[:, par, n, :, :], w_e[n][bass.ds(number, 1)].rearrange("e p c f -> (e p) c f")
                                 ).then_inc(ew_in[par], 16)
                if prev:
                    wait_alone(sp, ya_ready, nth(prev, 1))
                    if NCH > 2:
                        wait_alone(sp, yb_ready, nth(prev, 1))
                    store(prev, par, old)

            each_expert(sp, expert)
            for e in (E - 2, E - 1):
                sp.wait_ge(ya_ready, e + 1)
                if NCH > 2:
                    sp.wait_ge(yb_ready, e + 1)
                store((None, e), e % 2, e)

            def combine(s, par):
                w = stages(s)[0]
                if w:
                    prev = back(w, 2)
                    number = num(w)
                    if exists(prev):
                        wait_alone(sp, c_sum, nth(prev, 1))
                    sp.dma_start(xc[:, par, :, :], x1_w[bass.ds(number, 1)].rearrange("w p q f -> (w p) q f")
                                 ).then_inc(c_in[par], 16)

            steps(sp, combine)
            sp.wait_ge(c_out[0], 16 * (NW // 2))
            sp.wait_ge(c_out[1], 16 * (NW // 2))

        @block.gpsimd
        def _(pool):
            pool.memset(ident[:, :], 0.0)
            pool.memset(identb[:, :], 0.0)
            pool.memset(mask_g[:, :, :], 1.0)
            pool.memset(earlier[:, :], 1.0)
            pool.memset(onesb[:, :], 1.0)
            pool.memset(mhalf[:, :], -0.5)
            pool.iota(iota_e[:, :], pattern=[[1, E]], base=0, channel_multiplier=0, allow_small_or_imprecise_dtypes=True)
            pool.drain()
            for m in (ident, identb):
                pool.affine_select(out=m[:, :], in_=m[:, :], compare_op=ALU.not_equal, fill=1.0,
                                   base=0, pattern=[[-1, P]], channel_multiplier=1)
            for n in (0, 3):
                pool.affine_select(out=mask_g[:, n, :], in_=mask_g[:, n, :], compare_op=ALU.is_gt, fill=0.0,
                                   base=0, pattern=[[-1, P]], channel_multiplier=1)
            pool.memset(mask_g[:, 1, :], 0.0)
            pool.affine_select(out=earlier[:, :], in_=earlier[:, :], compare_op=ALU.is_gt, fill=0.0,
                               base=0, pattern=[[1, P]], channel_multiplier=-1)
            pool.drain().then_inc(const_pool, 1)

            def inv_std(n, w):
                wait(pool, ln_var[n], w)
                pool.tensor_tensor(rstd[:, n, :], ve[:, n, :], mhalf[:, :], ALU.pow).then_inc(ln_rstd[n], 1)

            def remainder(j, a):
                wait(pool, hi_ready, a, 4, j)
                if j < 2:
                    wait(pool, mid_ready, back(a), 4, j + 2)
                else:
                    wait(pool, mid_ready, a, 4, j - 2)
                pool.tensor_tensor(rest[:, j % 2, :], x32[:, j % 2, :], parts[:, j % 2, 0, :], ALU.subtract
                                   ).then_inc(rest_ready, 1)

            def low_part(j, a):
                wait(pool, mid_ready, a, 4, j)
                pool.tensor_tensor(parts[:, j % 2, 2, :], rest[:, j % 2, :], parts[:, j % 2, 1, :], ALU.subtract
                                   ).then_inc(lo_ready, 1)

            def step(s, par):
                a, c, d = stages(s)
                if a:
                    remainder(0, a)
                    remainder(1, a)
                    low_part(0, a)
                    low_part(1, a)
                    remainder(2, a)
                    remainder(3, a)
                if d:
                    inv_std(1, d)
                if a:
                    low_part(2, a)
                    low_part(3, a)
                if d:
                    wait(pool, n1_ready, d)
                    pool.tensor_tensor(ybuf[:, :, :], fbuf[:, :, :], gamma_row[:, :].unsqueeze(1).to_broadcast([P, 2, D]), ALU.mult)
                    pool.drain()
                    pool.tensor_tensor(ybuf[:, :, :], ybuf[:, :, :], beta_row[:, :].unsqueeze(1).to_broadcast([P, 2, D]), ALU.add
                                       ).then_inc(y_ready, 1)
                    inv_std(2, d)
                    wait(pool, z_ready, d)
                    if exists(back(d)):
                        pool.wait_ge(x1_out, nth(back(d), 16, 15))
                    wait(pool, xn2_ready, back(d))
                    pool.wait_ge(xr_in[par], xr_count(d))
                    pool.tensor_tensor(x1[:, :, :], ybuf[:, :, :], xr[:, par, :, :], ALU.add).then_inc(x1_ready, 1)
                    inv_std(3, d)
                    pool.wait_ge(zeroed, N_ZERO)
                    wait(pool, slot_ready, d)
                    for q in range(2):
                        pool.indirect_dma_start(
                            out=slots_d, out_offset=bass.IndirectOffsetOnAxis(ap=slot_u[:, par, q:q + 1], axis=0),
                            in_=xn2[:, q, :], in_offset=None, bounds_check=NSLOT - 1, oob_is_err=False).then_inc(scat, 16)
                nxt = back(s, -1)
                if a and (nxt[0] is not None or nxt[1] < NW):
                    inv_std(0, nxt)

            def xr_count(d):
                i, n = d
                n = 16 * (n // 2 + 1)
                return n if i is None else i * 16 + n

            inv_std(0, (None, 0))
            steps(pool, step)

            for par in range(2):
                pool.wait_ge(ye_out[par], 16 * NCH * E // 2)

            def combine(s, par):
                w, g, _ = stages(s)
                if w:
                    if exists(back(w, 2)):
                        wait_alone(pool, c_var, nth(back(w, 2), 1))
                    wait_alone(pool, c_idx, nth(w, 1))
                    for q in range(2):
                        pool.indirect_dma_start(
                            out=yg[:, par, q, :], out_offset=None, in_=y_d,
                            in_offset=bass.IndirectOffsetOnAxis(ap=slot_c[:, par, q:q + 1], axis=0),
                            bounds_check=NSLOT - 1, oob_is_err=False).then_inc(g_in[par], 16)
                if g:
                    if exists(back(g, 2)):
                        pool.wait_ge(c_out[1 - par], alternate(back(g, 2), 16))
                    pool.wait_ge(c_nrm, nth(g, 1))
                    pool.tensor_tensor(oc[:, 1 - par, :, :], zc[:, 1 - par, :, :], xc[:, 1 - par, :, :], ALU.add).then_inc(c_sum, 1)

            steps(pool, combine)

        @block.scalar
        def _(act):
            act.wait_ge(fus_sem, 1)
            act.activation(fus_e[:, :], fus[:, :], ACT.Exp, bias=fus_m[:, 0:1]).then_inc(fus_exp, 1)
            n = 0
            for b in range(2):
                for c in range(2):
                    act.wait_ge(w_fold, n + 1)
                    act.activation(weff[:, b, c, 0:512].rearrange("p (x d h) -> p x d h", d=HD, h=8),
                                   banks[2 * (n // 2 % 2)][:, :].rearrange("p (x h d) -> p x d h", d=HD, h=8), ACT.Copy)
                    act.wait_ge(w_fold, n + 2)
                    act.activation(weff[:, b, c, 512:768], banks[2 * (n // 2 % 2) + 1][:, 0:256], ACT.Copy).then_inc(w_fold_out, 1)
                    n += 2

            def exps(u, c):
                wait(act, s2_full, c, UNITS, u)
                if u < 8:
                    wait(act, pv_full, back(c), GROUPS, 6 + u // 4)
                elif u < 16:
                    wait(act, pv_full, c, GROUPS, (u - 8) // 2)
                else:
                    wait(act, pv_full, c, GROUPS, 4 + (u - 16) // 4)
                act.activation(pt[:, u % 8, :], S2[u % 2][:, :], ACT.Exp).then_inc(p_ready, 1)

            def values_out(g, c):
                wait(act, pv_full, c, GROUPS, g)
                b = g // 4
                wait(act, nrm_full[b], back(c), 2, 1)
                act.activation(OT[:, b, g % 4, :], PV[:, 0:WIN], ACT.Copy).then_inc(ot_ready, 1)

            def projected(j, a, par):
                wait(act, pj_full, a, 4, j)
                wait(act, rest_ready, a if j >= 2 else back(a), 4, (j - 2) % 4)
                b, qk = j // 2, j % 2
                bank = pj_bank(f"p{j}", par)
                for t in range(2):
                    last = act.activation(x32[:, j % 2, t * WIN:(t + 1) * WIN], bank[:, t * WIN:(t + 1) * WIN], ACT.Identity,
                                          bias=bqk[:, b, 2 * qk + t:2 * qk + t + 1], scale=QSCALE if qk == 0 else 1.0)
                last.then_inc(x32_ready, 1)

            def v_out(q, a, par):
                wait(act, v_full, a, 2, q)
                wait(act, pv_full, back(a, 2), GROUPS, GROUPS - 1)
                act.activation(v_pad[:, par, q, :, :, 0:HD],
                               pj_bank(f"v{q}", par)[:, :].rearrange("p (b h d) -> p b h d", b=2, d=HD), ACT.Copy
                               ).then_inc(v_ready, 1)

            def maxima_out(b, a):
                wait(act, mT_full[b], a)
                if exists(back(a)):
                    act.wait_ge(m_in[b], nth(back(a), 16, 15))
                act.activation(mT[:, b, :], TR[0:48, 0:WIN // 2].bitcast(bf16), ACT.Copy).then_inc(mT_ready[b], 1)

            def onT_out(b, w):
                wait(act, onT_full[b], w)
                wait(act, o_full, back(w))
                act.activation(OnT[:, b, :, :].rearrange("p t n -> p (t n)"), TR[:, :], ACT.Copy).then_inc(onT_ready[b], 1)

            def step(s, par):
                a, c, d = stages(s)
                for k in range(UNITS):
                    if c:
                        exps(k, c)
                        if k in (3, 5, 7, 9):
                            values_out((k - 3) // 2, c)
                        if k in (13, 17, 21):
                            values_out(4 + (k - 13) // 4, c)
                    if a:
                        if k == 0:
                            wait(act, xnT_full, a)
                            wait(act, v_full, back(a), 2, 1)
                            act.activation(xnT[:, :, :].rearrange("p c n -> p (c n)"), pj_bank("xnT", par)[:, :], ACT.Copy
                                           ).then_inc(xnT_ready, 1)
                        if k in (1, 2, 4, 5):
                            projected((1, 2, 4, 5).index(k), a, par)
                        if k in (3, 6):
                            v_out((3, 6).index(k), a, par)
                    if d and k == 4:
                        onT_out(1, d)
                    if c and k == 14:
                        onT_out(0, c)
                    if a and k == 15:
                        maxima_out(0, a)
                    if d and k == 18:
                        wait(act, x2T_full, d)
                        act.activation(xn2T[:, :, :].rearrange("p c n -> p (c n)"), TR[:, :], ACT.Copy).then_inc(x2T_ready, 1)
                    if d and k == 21:
                        wait(act, lg_ready, d)
                        for q in range(2):
                            last = act.activation(egate[:, q, :], lg[:, q, :], ACT.Exp, bias=ntop[:, q:q + 1],
                                                  accum_out=gsum[:, q:q + 1])
                        last.then_inc(gsum_ready, 1)
                if c:
                    values_out(7, c)
                if a:
                    maxima_out(1, a)

            steps(act, step)

            def transposed(e, par):
                act.wait_ge(eT_full, nth(e, 1))
                if ebefore(e, 2):
                    act.wait_ge(gu_full, nth(ebefore(e, 2), 2, 1))
                for c in range(2):
                    last = act.activation(eT[:, par, c, :], banks[c][:, 0:CAP], ACT.Copy)
                last.then_inc(eT_ready, 1)

            def expert(e, par):
                for m in range(2):
                    act.wait_ge(gu_full, nth(e, 2, m))
                    if ebefore(e):
                        act.wait_ge(h_ready, nth(ebefore(e), 2, m))
                    act.activation(sg[:, m, :], banks[2 + 2 * m][:, 0:CAP], ACT.Silu).then_inc(sg_ready, 1)
                if e[0] is not None or e[1] < E - 1:
                    transposed(back(e, -1), 1 - par)
                act.wait_ge(ye_full, nth(e, 1))
                if ebefore(e, 2):
                    act.wait_ge(ye_out[par], alternate(ebefore(e, 2), 16 * NCH))
                full = min(NCH, 2)
                rows = CHUNKS[0][1]
                act.activation(ybf[0:rows, par, 0:full, :].rearrange("p n f -> p (n f)"), banks[6][0:rows, 0:full * D], ACT.Copy
                               ).then_inc(ya_ready, 1)

            transposed((None, 0), 0)
            each_expert(act, expert)

            def combine(s, par):
                w, g, _ = stages(s)
                if w:
                    act.wait_ge(c_var, nth(w, 1))
                    act.activation(sd_c[:, par, :], ve_c[:, par, :], ACT.Sqrt).then_inc(c_std, 1)
                if g:
                    number = act.snap(num(g)) if g[0] is not None else num(g)
                    act.wait_ge(c_sum, nth(g, 1))
                    act.dma_start(out_w[bass.ds(number, 1)].rearrange("w p q f -> (w p) q f"), oc[:, 1 - par, :, :]
                                  ).then_inc(c_out[1 - par], 16)

            steps(act, combine)

        @block.vector
        def _(dve):
            dve.memset(zeros[:, :], 0.0)
            dve.memset(base[:, :], 0.0)
            dve.memset(v_pad[:, :, :, :, :, :], 0.0)
            dve.drain()
            for p_ in range(2):
                for q in range(2):
                    for b in range(2):
                        dve.memset(v_pad[:, p_, q, b, :, HD:HD + 1], 1.0)
            dve.drain().then_inc(const_dve, 1)
            dve.wait_ge(w_in, 16 * 16)
            dve.tensor_copy(bvb[:, :, :], bv[:, :].unsqueeze(2).to_broadcast([P, 4, P]))
            dve.reduce_max(fus_m[:, 1:2], fus[:, :], AX.X)
            dve.tensor_scalar(bqk[:, :, 0:2], bqk[:, :, 0:2], QSCALE, None, ALU.mult)
            dve.drain()
            dve.tensor_scalar(fus_m[:, 0:1], fus_m[:, 1:2], -1.0, None, ALU.mult).then_inc(fus_sem, 1)
            dve.wait_ge(fus_exp, 1)
            dve.reduce_sum(fus_m[:, 1:2], fus_e[:, :], AX.X)
            dve.drain()
            dve.reciprocal(fus_m[:, 1:2], fus_m[:, 1:2])
            dve.drain()
            dve.tensor_scalar(fus_e[:, :], fus_e[:, :], fus_m[:, 1:2], None, ALU.mult)
            dve.drain()
            for b in range(2):
                dve.tensor_scalar(wo[:, 2 * b:2 * b + 2, :], wo[:, 2 * b:2 * b + 2, :], fus_e[:, b:b + 1], None, ALU.mult)
                dve.tensor_scalar(bo[:, b, :], bo[:, b, :], fus_e[:, b:b + 1], None, ALU.mult)
            dve.drain()
            dve.tensor_tensor(bias_row[:, :], bo[:, 0, :], bo[:, 1, :], ALU.add).then_inc(wo_ready, 1)
            dve.wait_ge(bias_ps, 1)
            dve.drain()
            dve.tensor_tensor(bias_row[:, :], TR[:, 0:D], bias_row[:, :], ALU.add)
            dve.wait_ge(w_fold, 8)
            dve.wait_ge(zeroed, N_ZERO)
            for p_ in range(2):
                for b in range(2):
                    dve.memset(stack[NPART:KROWS, p_, b, 1, :, :, :].rearrange("r h t n -> r (h t n)"), 1.0)
            dve.drain().then_inc(const_dve, 1)

            def stats(n, src, w):
                for q in range(2):
                    dve.bn_stats(bst[:, n, q, :], src[:, q, :])
                dve.drain()
                for q in range(2):
                    dve.bn_aggr(mv[:, n, q, :], bst[:, n, q, :])
                dve.drain()
                dve.tensor_scalar(ve[:, n, :], mv[:, n, :, 1], EPS, None, ALU.add).then_inc(ln_var[n], 1)

            def norm(n, dst, src, sem, w):
                wait(dve, ln_rstd[n], w)
                for q in range(2):
                    last = dve.tensor_scalar(dst[:, q, :], src[:, q, :], mv[:, n, q, 0:1], rstd[:, n, q:q + 1],
                                             ALU.subtract, ALU.mult)
                last.then_inc(sem, 1)

            def first_norm(w, par):
                i, n = w
                n = 16 * (n // 2 + 1)
                dve.wait_ge(x_in[par], n if i is None else i * 16 + n)
                stats(0, xw[:, par, :, :], w)
                wait(dve, xnT_full, back(w))
                norm(0, xn, xw[:, par, :, :], xn_ready, w)

            def high_part(j, a):
                wait(dve, x32_ready, a, 4, j)
                w, j2 = (a, j - 2) if j >= 2 else (back(a), j + 2)
                if exists(w):
                    dve.wait_ge(spread[j2], nth(w, 96, 95))
                dve.tensor_copy(parts[:, j % 2, 0, :], x32[:, j % 2, :]).then_inc(hi_ready, 1)

            def mid_part(j, a):
                wait(dve, rest_ready, a, 4, j)
                dve.tensor_copy(parts[:, j % 2, 1, :], rest[:, j % 2, :]).then_inc(mid_ready, 1)

            def maximum(u, a):
                wait(dve, s1_full, a, UNITS, u)
                if u < LU:
                    dst = mx[:, 0, :, :].rearrange("p q (h t) -> p t h q", t=2)[:, u // 4, (2 * u) % 8:(2 * u) % 8 + 2, :]
                    src = S1[u % 2][:, :].rearrange("p (h q n) -> p h q n", h=2, q=2)
                else:
                    h = u - LU
                    dst = mx[:, 1, :, 2 * (h % 8) + h // 8]
                    src = S1[u % 2][:, :].rearrange("p (q n) -> p q n", q=2)
                dve.reduce_max(dst, src, AX.X).then_inc(s1_read, 1)

            def split_maxima(b, a):
                dve.drain()
                wait(dve, mT_full[b], back(a))
                dve.tensor_scalar(mparts[:, b, :, 0, :], mx[:, b, :, :], -1.0, None, ALU.mult)
                dve.drain()
                dve.scalar_tensor_tensor(mneg[:, b, :, :], mx[:, b, :, :], -1.0, mparts[:, b, :, 0, :], ALU.mult, ALU.subtract)
                dve.drain()
                dve.tensor_copy(mparts[:, b, :, 1, :], mneg[:, b, :, :])
                dve.drain()
                dve.tensor_tensor(mparts[:, b, :, 2, :], mneg[:, b, :, :], mparts[:, b, :, 1, :], ALU.subtract
                                  ).then_inc(mparts_ready[b], 1)

            def normalise(b, q, w):
                wait(dve, nrm_full[b], w, 2, q)
                src = TR[:, :].rearrange("p (h m) -> p h m", m=32)
                dve.reciprocal(rden[:, b, :], src[:, :, HD])
                dve.drain()
                wait(dve, onT_full[b], back(w))
                dve.tensor_tensor(On[:, b, q, :].rearrange("p (h d) -> p h d", d=HD), src[:, :, 0:HD],
                                  rden[:, b, :].unsqueeze(2).to_broadcast([P, NH, HD]), ALU.mult).then_inc(on_ready[b], 1)

            def route_top(d):
                wait(dve, lg_full, d)
                wait(dve, gsum_ready, back(d))
                dve.tensor_copy(lg[:, :, :], TR[:, 0:2 * E].rearrange("p (q e) -> p q e", q=2))
                dve.drain()
                for q in range(2):
                    dve.max(top[:, q, :], lg[:, q, :])
                dve.drain()
                dve.tensor_scalar(ntop[:, :], top[:, :, 0], -1.0, None, ALU.mult).then_inc(lg_ready, 1)
                for q in range(2):
                    dve.max_index(top_i[:, q, :], top[:, q, :], lg[:, q, :])
                dve.drain()
                dve.tensor_copy(idx_f[:, :], top_i[:, :, 0])
                dve.drain()
                wait(dve, cs_full, back(d))
                for q in range(2):
                    last = dve.tensor_scalar(hot[:, q, :], iota_e[:, :], idx_f[:, q:q + 1], None, ALU.is_equal)
                last.then_inc(hot_ready, 1)

            def route_slot(d, par):
                wait(dve, cs_full, d)
                dve.tensor_tensor(pos[:, :, :], TR[:, 0:2 * E].rearrange("p (q e) -> p q e", q=2),
                                  base[:, :].unsqueeze(1).to_broadcast([P, 2, E]), ALU.add)
                wait(dve, gsum_ready, d)
                dve.reciprocal(gate1[:, :], gsum[:, :])
                dve.drain()
                dve.tensor_tensor(base[:, :], TR[:, 2 * E:3 * E], base[:, :], ALU.add).then_inc(cs_read, 1)
                dve.tensor_tensor(posh[:, :, :], pos[:, :, :], hot[:, :, :], ALU.mult)
                dve.drain()
                dve.reduce_sum(pos1[:, :], posh[:, :, :], AX.X)
                dve.drain()
                dve.tensor_scalar(okf[:, :], pos1[:, :], float(CAP), None, ALU.is_lt)
                dve.scalar_tensor_tensor(slotf[:, :], idx_f[:, :], float(CAP), pos1[:, :], ALU.mult, ALU.add)
                dve.drain()
                dve.tensor_scalar(far[:, :], okf[:, :], -float(4 * NSLOT), float(4 * NSLOT), ALU.mult, ALU.add)
                dve.tensor_tensor(gate_all[:, bass.ds(num(d), 1), :].rearrange("p w q -> p (w q)"), gate1[:, :], okf[:, :], ALU.mult)
                dve.tensor_scalar(slot_all[:, bass.ds(num(d), 1), :].rearrange("p w q -> p (w q)"), slotf[:, :],
                                  float(NSLOT - 1), None, ALU.min)
                dve.drain()
                if exists(back(d, 2)):
                    dve.wait_ge(scat, nth(back(d, 2), 32, 31))
                dve.tensor_tensor(slot_u[:, par, :], slotf[:, :], far[:, :], ALU.add).then_inc(slot_ready, 1)

            def step(s, par):
                a, c, d = stages(s)
                S1_AT = {8: (0, 1), 9: (2, 3), 10: (4, 5), 11: (6, 7), 12: (8, 9), 13: (10, 11), 14: (12, 13), 15: (14, 15)}
                for k in range(UNITS):
                    if d and k in (1, 2):
                        normalise(1, k - 1, d)
                    if a:
                        if k == 1:
                            high_part(0, a)
                        if k == 2:
                            mid_part(0, a)
                            high_part(1, a)
                        if k == 3:
                            mid_part(1, a)
                        if k == 4:
                            high_part(2, a)
                        if k == 5:
                            mid_part(2, a)
                            high_part(3, a)
                    if d and k == 5:
                        wait(dve, o_full, d)
                        wait(dve, y_ready, back(d))
                        dve.tensor_tensor(fbuf[:, :, :], TR[:, :].rearrange("p (q f) -> p q f", q=2),
                                          bias_row[:, :].unsqueeze(1).to_broadcast([P, 2, D]), ALU.add).then_inc(f_ready, 1)
                        dve.drain()
                        stats(1, fbuf, d)
                    if a and k == 6:
                        mid_part(3, a)
                    if d and k == 7:
                        norm(1, fbuf, fbuf, n1_ready, d)
                    if a and k >= 8:
                        for u in S1_AT.get(k, (k,)):
                            maximum(u, a)
                    if d and k == 8:
                        wait(dve, y_ready, d)
                        stats(2, ybuf, d)
                    if d and k == 10:
                        norm(2, ybuf, ybuf, z_ready, d)
                    if c and k in (11, 12):
                        normalise(0, k - 11, c)
                    if a and k == 12:
                        split_maxima(0, a)
                    if d and k == 12:
                        wait(dve, x1_ready, d)
                        stats(3, x1, d)
                    if d and k == 14:
                        if exists(back(d)):
                            dve.wait_ge(scat, nth(back(d), 32, 31))
                        norm(3, xn2, x1, xn2_ready, d)
                        dve.tensor_copy(st_all[:, bass.ds(num(d), 1), 0:2].rearrange("p w q -> p (w q)"), mv[:, 3, :, 0])
                        dve.tensor_copy(st_all[:, bass.ds(num(d), 1), 2:4].rearrange("p w q -> p (w q)"), rstd[:, 3, :])
                    if d and k == 20:
                        route_top(d)
                    if d and k == 22:
                        route_slot(d, par)
                nxt = back(s, -1)
                if a and (nxt[0] is not None or nxt[1] < NW):
                    first_norm(nxt, 1 - par)
                if a:
                    split_maxima(1, a)

            first_norm((None, 0), 0)
            steps(dve, step)

            def expert(e, par):
                for m in range(2):
                    dve.wait_ge(sg_ready, nth(e, 2, m))
                    if ebefore(e, 2):
                        dve.wait_ge(ye_full, nth(ebefore(e, 2), 1))
                    dve.tensor_tensor(hT[:, par, m, :], banks[3 + 2 * m][:, 0:CAP], sg[:, m, :], ALU.mult).then_inc(h_ready, 1)
                if NCH > 2:
                    rows = CHUNKS[2][1]
                    dve.wait_ge(ye_full, nth(e, 1))
                    if ebefore(e, 2):
                        dve.wait_ge(ye_out[par], alternate(ebefore(e, 2), 16 * NCH))
                    dve.tensor_copy(ybf[0:rows, par, 2, :], banks[7][0:rows, 0:D]).then_inc(yb_ready, 1)

            each_expert(dve, expert)

            def numbers(w, par):
                if exists(back(w, 2)):
                    dve.wait_ge(g_in[par], alternate(back(w, 2), 32))
                dve.tensor_copy(slot_c[:, par, :], slot_all[:, bass.ds(num(w), 1), :].rearrange("p w q -> p (w q)")).then_inc(c_idx, 1)

            def combine(s, par):
                w, g, _ = stages(s)
                nxt = back(s, -1)
                if w:
                    if nxt[0] is not None or nxt[1] < NW:
                        numbers(nxt, 1 - par)
                    dve.wait_ge(c_in[par], alternate(w, 16))
                    for q in range(2):
                        dve.tensor_scalar(xn2c[:, q, :], xc[:, par, q, :], st_all[:, bass.ds(num(w), 1), q],
                                          st_all[:, bass.ds(num(w), 1), 2 + q], ALU.subtract, ALU.mult)
                    dve.drain()
                    dve.wait_ge(g_in[par], alternate(w, 32))
                    if exists(back(w, 2)):
                        dve.wait_ge(c_sum, nth(back(w, 2), 1))
                    for q in range(2):
                        dve.scalar_tensor_tensor(zc[:, par, q, :], yg[:, par, q, :], gate_all[:, bass.ds(num(w), 1), q],
                                                 xn2c[:, q, :], ALU.mult, ALU.add)
                    dve.drain()
                    for q in range(2):
                        dve.bn_stats(bst_c[:, q, :], zc[:, par, q, :])
                    dve.drain()
                    for q in range(2):
                        dve.bn_aggr(mv_c[:, par, q, :], bst_c[:, q, :])
                    dve.drain()
                    dve.tensor_scalar(ve_c[:, par, :], mv_c[:, par, :, 1], EPS, None, ALU.add).then_inc(c_var, 1)
                if g:
                    dve.wait_ge(c_std, nth(g, 1))
                    dve.reciprocal(rs_c[:, 1 - par, :], sd_c[:, 1 - par, :])
                    dve.drain()
                    for q in range(2):
                        last = dve.tensor_scalar(zc[:, 1 - par, q, :], zc[:, 1 - par, q, :], mv_c[:, 1 - par, q, 0:1], rs_c[:, 1 - par, q:q + 1],
                                                 ALU.subtract, ALU.mult)
                    last.then_inc(c_nrm, 1)

            numbers((None, 0), 0)
            steps(dve, combine)

        @block.tensor
        def _(pe):
            pe.wait_ge(w_in, 16 * 16)
            n = 0
            for b in range(2):
                for c in range(2):
                    if n >= 4:
                        pe.wait_ge(w_fold_out, n // 2 - 1)
                    for half, (lo, width) in enumerate(((0, 512), (512, 256))):
                        for kc in range(2):
                            last = pe.matmul(banks[2 * (n // 2 % 2) + half][:, 0:width], pT[:, b, kc, c * P:(c + 1) * P],
                                             winT[:, b, kc, lo:lo + width], start=(kc == 0), stop=(kc == 1))
                        last.then_inc(w_fold, 1)
                    n += 2
            pe.wait_ge(wo_ready, 1)
            for c in range(4):
                last = pe.matmul(TR[:, 0:D], bvb[:, c, :], wo[:, c, :], start=(c == 0), stop=(c == 3))
            last.then_inc(bias_ps, 1)
            pe.wait_ge(const_pool, 1)
            pe.wait_ge(w_fold_out, 4)
            pe.wait_ge(const_dve, 2)

            def scores(u, c, par):
                if u == 0:
                    for j in (0, 1):
                        pe.wait_ge(spread[j], nth(c, 96, 95))
                    pe.wait_ge(m_in[0], nth(c, 16, 15))
                if u == LU:
                    for j in (2, 3):
                        pe.wait_ge(spread[j], nth(c, 96, 95))
                    pe.wait_ge(m_in[1], nth(c, 16, 15))
                if u >= 2:
                    wait(pe, p_ready, c, UNITS, u - 2)
                else:
                    wait(pe, p_ready, back(c), UNITS, UNITS - 2 + u)
                bank = S2[u % 2]
                if u < LU:
                    pe.matmul(bank[:, :], identb[:, :], tri.unsqueeze(1).to_broadcast([P, 4, P]), start=True, stop=False)
                    for h2 in range(2):
                        for j in range(2):
                            h = 2 * u + h2
                            last = pe.matmul(bank[:, (2 * h2 + j) * P:(2 * h2 + j + 1) * P], k_stack(par, 0, h, j * P, P),
                                             q_stack(par, 0, h, j * P, P), start=False, stop=(h2 == 1 and j == 1))
                else:
                    pe.matmul(bank[:, :], identb[:, :], mask_g[:, :, :].rearrange("p a n -> p (a n)"), start=True, stop=False)
                    for kb in range(2):
                        last = pe.matmul(bank[:, kb * WIN:(kb + 1) * WIN], k_stack(par, 1, u - LU, kb * P, P),
                                         q_stack(par, 1, u - LU, 0, WIN), start=False, stop=(kb == 1))
                last.then_inc(s2_full, 1)

            def values(g, c, par):
                wait(pe, ot_ready, c if g else back(c), GROUPS, (g - 1) % GROUPS)
                if g < 4:
                    wait(pe, p_ready, c, UNITS, 2 * g + 1)
                    for j in range(2):
                        for h4 in range(4):
                            last = pe.matmul(PV[32 * h4:32 * h4 + 32, j * P:(j + 1) * P], v_pad[:, par, j, 0, 4 * g + h4, :],
                                             pt[:, (2 * g + h4 // 2) % 8, (2 * (h4 % 2) + j) * P:(2 * (h4 % 2) + j + 1) * P],
                                             start=True, stop=True)
                else:
                    u0 = LU + 4 * (g - 4)
                    wait(pe, p_ready, c, UNITS, u0 + 3)
                    for kb in range(2):
                        for h4 in range(4):
                            last = pe.matmul(PV[32 * h4:32 * h4 + 32, 0:WIN], v_pad[:, par, kb, 1, 4 * (g - 4) + h4, :],
                                             pt[:, (u0 + h4) % 8, kb * WIN:(kb + 1) * WIN], start=(kb == 0), stop=(kb == 1))
                last.then_inc(pv_full, 1)

            def project(j, a, s, par):
                wait_read(pe, PJ_USES, f"p{j}", s, 2)
                bank, b, qk = pj_bank(f"p{j}", par), j // 2, j % 2
                for t in range(2):
                    for c in range(2):
                        last = pe.matmul(bank[:, t * WIN:(t + 1) * WIN], weff[:, b, c, qk * D + t * P:qk * D + (t + 1) * P],
                                         xnT[:, c, :], start=(c == 0), stop=(c == 1))
                last.then_inc(pj_full, 1)

            def project_v(q, a, s, par):
                wait_read(pe, PJ_USES, f"v{q}", s, 2)
                for c in range(2):
                    last = pe.matmul(pj_bank(f"v{q}", par)[:, :], xnT[:, c, q * P:(q + 1) * P], weff[:, :, c, 2 * D:3 * D],
                                     start=(c == 0), stop=(c == 1))
                last.then_inc(v_full, 1)

            def row_scores(u, a, par):
                if u == 0:
                    for j in (0, 1):
                        pe.wait_ge(spread[j], nth(a, 96, 95))
                if u == LU:
                    for j in (2, 3):
                        pe.wait_ge(spread[j], nth(a, 96, 95))
                if u >= 2:
                    wait(pe, s1_read, a, UNITS, u - 2)
                else:
                    wait(pe, s1_read, back(a), UNITS, UNITS - 2 + u)
                bank = S1[u % 2]
                for n in range(2):
                    for j in range(2):
                        if u < LU:
                            last = pe.matmul(bank[:, (2 * n + j) * P:(2 * n + j + 1) * P], q_stack(par, 0, 2 * u + n, j * P, P, NPART),
                                             k_stack(par, 0, 2 * u + n, j * P, P, NPART), start=True, stop=True)
                        elif j == 0:
                            last = pe.matmul(bank[:, n * WIN:(n + 1) * WIN], q_stack(par, 1, u - LU, n * P, P, NPART),
                                             k_stack(par, 1, u - LU, 0, WIN, NPART), start=True, stop=True)
                last.then_inc(s1_full, 1)

            def four_transposes(src, sem_full):
                for n in range(4):
                    last = pe.transpose(TR[:, n * P:(n + 1) * P], src(n), ident[:, :])
                last.then_inc(sem_full, 1)

            def maxima_T(b, a, s):
                pe.wait_ge(const_pool, 1)
                wait_read(pe, TR_USES, ("mT_l", "mT_g")[b], s, 1)
                wait(pe, mparts_ready[b], a)
                trb = TR[:, :].bitcast(bf16)
                for q in range(2):
                    last = pe.transpose(trb[0:48, q * P:(q + 1) * P], mparts[:, b, q, :, :].rearrange("p r h -> p (r h)"), identb[:, :])
                last.then_inc(mT_full[b], 1)

            def norm_T(b, q, w, s):
                wait_read(pe, TR_USES, f"n_{'lg'[b]}{q}", s, 1)
                wait(pe, ot_ready, w, GROUPS, 3 + 4 * b)
                four_transposes(lambda n: OT[:, b, n, q * P:(q + 1) * P], nrm_full[b])

            def out_T(b, w, s):
                wait_read(pe, TR_USES, f"oT_{'lg'[b]}", s, 1)
                wait(pe, on_ready[b], w, 2, 1)
                four_transposes(lambda n: On[:, b, n % 2, n // 2 * P:(n // 2 + 1) * P], onT_full[b])

            def step(s, par):
                a, c, d = stages(s)
                S1_AT = {8: (0, 1), 9: (2, 3), 10: (4, 5), 11: (6, 7), 12: (8, 9), 13: (10, 11), 14: (12, 13), 15: (14, 15)}
                for k in range(UNITS):
                    if c:
                        scores(k, c, 1 - par)
                        if k in (3, 5, 7, 9):
                            values((k - 3) // 2, c, 1 - par)
                        if k in (13, 17, 21):
                            values(4 + (k - 13) // 4, c, 1 - par)
                    if a:
                        if k == 0:
                            wait_read(pe, PJ_USES, "xnT", s, 2)
                            wait(pe, xn_ready, a)
                            bank = pj_bank("xnT", par)
                            for n in range(4):
                                last = pe.transpose(bank[:, n * P:(n + 1) * P], xn[:, n % 2, n // 2 * P:(n // 2 + 1) * P], ident[:, :])
                            last.then_inc(xnT_full, 1)
                        if k == 1:
                            wait(pe, xnT_ready, a)
                        if k in (1, 2, 4, 5):
                            project((1, 2, 4, 5).index(k), a, s, par)
                        if k in (3, 6):
                            project_v((3, 6).index(k), a, s, par)
                    if d:
                        if k in (1, 2):
                            norm_T(1, k - 1, d, s)
                        if k == 4:
                            out_T(1, d, s)
                        if k == 5:
                            wait_read(pe, TR_USES, "op", s, 1)
                            wait(pe, onT_ready[0], d)
                            wait(pe, onT_ready[1], d)
                            for q in range(2):
                                for n in range(4):
                                    last = pe.matmul(TR[:, q * D:(q + 1) * D], OnT[:, n // 2, n % 2, q * P:(q + 1) * P], wo[:, n, :],
                                                     start=(n == 0), stop=(n == 3))
                            last.then_inc(o_full, 1)
                    if c:
                        if k in (11, 12):
                            norm_T(0, k - 11, c, s)
                        if k == 14:
                            out_T(0, c, s)
                    if a and k == 15:
                        maxima_T(0, a, s)
                    if a and k >= 8:
                        for u in S1_AT.get(k, (k,)):
                            row_scores(u, a, par)
                    if d:
                        if k == 18:
                            wait_read(pe, TR_USES, "x2T", s, 1)
                            wait(pe, xn2_ready, d)
                            four_transposes(lambda n: xn2[:, n % 2, n // 2 * P:(n // 2 + 1) * P], x2T_full)
                        if k == 20:
                            wait_read(pe, TR_USES, "lg", s, 1)
                            wait(pe, x2T_ready, d)
                            for q in range(2):
                                for n in range(2):
                                    last = pe.matmul(TR[:, q * E:(q + 1) * E], xn2T[:, n, q * P:(q + 1) * P], wr[:, n, :],
                                                     start=(n == 0), stop=(n == 1))
                            last.then_inc(lg_full, 1)
                        if k == 22:
                            wait_read(pe, TR_USES, "cs", s, 1)
                            wait(pe, hot_ready, d)
                            pe.matmul(TR[:, 0:E], earlier[:, :], hot[:, 0, :], start=True, stop=True)
                            pe.matmul(TR[:, E:2 * E], earlier[:, :], hot[:, 1, :], start=True, stop=False)
                            pe.matmul(TR[:, E:2 * E], onesb[:, :], hot[:, 0, :], start=False, stop=True)
                            pe.matmul(TR[:, 2 * E:3 * E], onesb[:, :], hot[:, 0, :], start=True, stop=False)
                            pe.matmul(TR[:, 2 * E:3 * E], onesb[:, :], hot[:, 1, :], start=False, stop=True).then_inc(cs_full, 1)
                if c:
                    values(7, c, 1 - par)
                if a:
                    maxima_T(1, a, s)

            steps(pe, step)

            def transposes(e, par):
                pe.wait_ge(er_in[par], alternate(e, 16 * NCH))
                if ebefore(e):
                    pe.wait_ge(eT_ready, nth(ebefore(e), 1))
                for c in range(2):
                    for n, (r, m) in enumerate(CHUNKS):
                        last = pe.transpose(banks[c][:, r:r + m], erows[0:m, par, n, c * P:(c + 1) * P], ident[0:m, 0:m])
                last.then_inc(eT_full, 1)

            def expert(e, par):
                pe.wait_ge(ew_in[par], alternate(e, 48))
                pe.wait_ge(eT_ready, nth(e, 1))
                for m in range(2):
                    if ebefore(e):
                        pe.wait_ge(h_ready, nth(ebefore(e), 2, m))
                    for n in range(2):
                        for c in range(2):
                            last = pe.matmul(banks[2 + 2 * m + n][:, 0:CAP], ew[:, par, n, c, m * P:(m + 1) * P], eT[:, par, c, :],
                                             start=(c == 0), stop=(c == 1))
                    last.then_inc(gu_full, 1)
                if e[0] is not None or e[1] < E - 1:
                    transposes(back(e, -1), 1 - par)
                if ebefore(e):
                    pe.wait_ge(ya_ready, nth(ebefore(e), 1))
                    if NCH > 2:
                        pe.wait_ge(yb_ready, nth(ebefore(e), 1))
                pe.wait_ge(h_ready, nth(e, 2, 1))
                for n, (r, m) in enumerate(CHUNKS):
                    for c in range(2):
                        last = pe.matmul(banks[6 + n // 2][0:m, n % 2 * D:(n % 2 + 1) * D], hT[:, par, c, r:r + m], ew[:, par, 2, c, :],
                                         start=(c == 0), stop=(c == 1))
                last.then_inc(ye_full, 1)

            pe.wait_ge(cs_read, NW)
            transposes((None, 0), 0)
            each_expert(pe, expert)


def kernel(**inputs):
    import numpy as np
    import concourse.bacc as bacc
    from concourse.bass_utils import run_bass_kernel_spmd

    arrays = layouts(inputs)
    shape = arrays["x"].shape
    nc = bacc.Bacc("TRN2", target_bir_lowering=False, num_devices=1)
    args = {}
    for name, a in arrays.items():
        args[name] = nc.dram_tensor(name, a.shape, mybir.dt.from_np(a.dtype), kind="ExternalInput").ap()
    args["out"] = nc.dram_tensor("out", shape, mybir.dt.float32, kind="ExternalOutput").ap()
    attention_moe_program(nc, shape[0] * shape[1], **args)
    r = run_bass_kernel_spmd(nc, [arrays], core_ids=[0])
    return r.results[0]["out"]


def layouts(inputs):
    import numpy as np
    a = {n.split("_", 2)[2]: np.ascontiguousarray(v) for n, v in inputs.items()}
    out = {"x": a["x"]}
    for b, name in (("l", "local"), ("g", "global")):
        bias = a[f"b{b}_in"]
        out[f"pT_{b}"] = np.ascontiguousarray(a[f"proj_{name}"].T)
        out[f"winT_{b}"] = np.ascontiguousarray(a[f"W{b}_in"].T)
        out[f"woT_{b}"] = np.ascontiguousarray(a[f"W{b}_out"].T)
        out[f"bqk_{b}"] = np.ascontiguousarray(bias[:512].reshape(2, 2, 8, 16).transpose(3, 2, 0, 1).reshape(128, 4))
        out[f"bv_{b}"] = np.ascontiguousarray(bias[512:].reshape(2, 128).T)
        out[f"bo_{b}"] = a[f"b{b}_out"]
    out["fusion_w"] = a["fusion_w"]
    out["gamma"] = a["ln_gamma"]
    out["beta"] = a["ln_beta"]
    for n in ("w_router", "w_gate", "w_up", "w_down"):
        out[n] = a[n]
    return out
```

```python
import concourse.bass as bass
from concourse import mybir
from contextlib import ExitStack

E_PARTS_Q = (0, 0, 0, 1, 1, 2)
E_PARTS_K = (0, 1, 2, 0, 1, 0)


def attention_moe_program(nc, T, x, pT_l, pT_g, winT_l, winT_g, woT_l, woT_g, bqk_l, bqk_g, bv_l, bv_g,
                          bo_l, bo_g, fusion_w, gamma, beta, w_router, w_gate, w_up, w_down, out):
    f32, bf16, u32 = mybir.dt.float32, mybir.dt.bfloat16, mybir.dt.uint32
    ALU, ACT, AX = mybir.AluOpType, mybir.ActivationFunctionType, mybir.AxisListType

    P = 128
    D = 256
    NH, HD = 16, 16
    WIN = 256
    NW = T // WIN
    E = 32
    CAP = -(-5 * T // (4 * E))
    NSLOT = E * CAP
    EPS = 1e-5
    QSCALE = 0.25
    UNITS = 24
    LU = 8
    GROUPS = 8
    NPART = 6 * HD
    KROWS = NPART + 3
    BROW = KROWS + 1
    CHUNKS = [(r, min(P, CAP - r)) for r in range(0, CAP, P)]
    NCH = len(CHUNKS)
    ROW = D + 4
    MEAN, RSTD, GATE, TOKEN = D, D + 1, D + 2, D + 3
    PIECES = [p_ for p_ in ((0, CAP // P, P), (CAP // P, 1, CAP % P)) if p_[1] * p_[2]]
    ZDMAS = 5
    ZREP = -(-NSLOT // P // ZDMAS)
    RING = 6

    def nth(w, per, k=0):
        i, c = w
        n = c * per + k + 1
        return n if i is None else i * (2 * per) + n

    def back(w, n=1):
        return (w[0], w[1] - n)

    def exists(w):
        return w[0] is not None or 0 <= w[1] < NW

    def num(w):
        return w[1] if w[0] is None else w[0] * 2 + w[1]

    def wait(eng, sem, w, per=1, k=0):
        if exists(w):
            eng.wait_ge(sem, nth(w, per, k))

    x_w = x.rearrange("b s f -> (b s) f").rearrange("(w q p) f -> w p q f", q=2, p=P)
    out_w = out.rearrange("b s f -> (b s) f").rearrange("(w q p) f -> w p q f", q=2, p=P)
    out_t = out.rearrange("b s f -> (b s) f")
    slots_d = nc.dram_tensor("slots_scratch", [NSLOT, ROW], f32).ap()

    with ExitStack() as ctx:
        def sb(name, shape, dt=f32, on=ctx):
            return on.enter_context(nc.sbuf_tensor(name, shape, dt))

        def sem(name):
            return ctx.enter_context(nc.semaphore(name))

        ident = sb("ident", [P, P])
        identb = sb("identb", [P, P], bf16)
        tri = sb("tri", [P, P], bf16)
        earlier = sb("earlier", [P, P], bf16)
        onesb = sb("onesb", [P, P], bf16)
        iota_e = sb("iota_e", [P, E])
        mhalf = sb("mhalf", [P, 4])
        weff = sb("weff", [P, 2, 2, 3 * D])
        wo = sb("wo", [P, 4, D])
        bqk = sb("bqk", [P, 2, 4])
        bias_row = sb("bias_row", [P, D])
        gamma_row = sb("gamma_row", [P, D])
        beta_row = sb("beta_row", [P, D])
        wr = sb("wr", [P, 2, E])
        zeros = sb("zeros", [P, ROW])
        ew = sb("ew", [P, 3, 3, 2, D])
        mv_e = sb("mv_e", [P, 2, NCH, 2])
        ve_e = sb("ve_e", [P, 2, NCH])
        rs_e = sb("rs_e", [P, 2, NCH])
        v_pad = sb("v_pad", [P, 2, 2, 2, NH, 32])
        xw = sb("xw", [P, 2, 2, D])
        xr = sb("xr", [P, 2, 2, D])
        xn = sb("xn", [P, 2, D])
        xnT = sb("xnT", [P, 2, WIN])
        x32 = sb("x32", [P, 2, 512])
        rest = sb("rest", [P, 2, 512])
        parts = sb("parts", [P, 4, 3, 512], bf16)
        mx = sb("mx", [P, 2, 2, NH])
        mneg = sb("mneg", [P, 2, 2, NH])
        mparts = sb("mparts", [P, 2, 2, 3, NH], bf16)
        mT = sb("mT", [48, 2, WIN], bf16)
        OT = sb("OT", [P, 2, 4, WIN])
        rden = sb("rden", [P, 2, NH])
        On = sb("On", [P, 2, 2, D])
        OnT = sb("OnT", [P, 2, 2, WIN])
        fbuf = sb("fbuf", [P, 2, D])
        ybuf = sb("ybuf", [P, 2, D])
        xrow = sb("xrow", [P, 2, ROW])
        x1 = xrow[:, :, 0:D]
        left = sb("left", [P, 2])
        obuf = sb("obuf", [P, 2, D])
        xn2 = sb("xn2", [P, 2, D])
        xn2T = sb("xn2T", [P, 2, WIN])
        bst = sb("bst", [P, 5, 2, 6])
        mv = sb("mv", [P, 5, 2, 2])
        ve = sb("ve", [P, 5, 2])
        rstd = sb("rstd", [P, 5, 2])
        lg = sb("lg", [P, 2, E])
        top = sb("top", [P, 2, 8])
        top_i = sb("top_i", [P, 2, 8], u32)
        ntop = sb("ntop", [P, 2])
        idx_f = sb("idx_f", [P, 2])
        hot = sb("hot", [P, 2, E], bf16)
        egate = sb("egate", [P, 2, E])
        gsum = sb("gsum", [P, 2])
        base = sb("base", [P, E])
        pos = sb("pos", [P, 2, E])
        posh = sb("posh", [P, 2, E])
        pos1 = sb("pos1", [P, 2])
        okf = sb("okf", [P, 2])
        slotf = sb("slotf", [P, 2])
        far = sb("far", [P, 2])
        gate1 = sb("gate1", [P, 2])
        slot_u = sb("slot_u", [P, 2], u32)
        with ExitStack() as prep:
            pT = sb("pT", [P, 2, 2, D], on=prep)
            winT = sb("winT", [P, 2, 2, 3 * D], on=prep)
            bv = sb("bv", [P, 4], on=prep)
            bvb = sb("bvb", [P, 4, P], on=prep)
            bo = sb("bo", [P, 2, D], on=prep)
            fus = sb("fus", [P, 2], on=prep)
            fus_e = sb("fus_e", [P, 2], on=prep)
            fus_m = sb("fus_m", [P, 2], on=prep)
        with ExitStack() as attn:
            pt = sb("pt", [P, 8, 512], on=attn)
            stack = sb("stack", [P, 2, 2, 2, 8, 2, WIN], bf16, on=attn)
        with ExitStack() as experts:
            erows = sb("erows", [P, RING, NCH, ROW], on=experts)
            zb = sb("zb", [P, RING, NCH, D], on=experts)
            idx_e = sb("idx_e", [P, RING, NCH], u32, on=experts)
            eT = sb("eT", [P, 2, 2, CAP], on=experts)
            sg = sb("sg", [P, 2, CAP], on=experts)
            hT = sb("hT", [P, 2, 2, CAP], on=experts)
            bst_e = sb("bst_e", [P, NCH, 6], on=experts)

        banks = [ctx.enter_context(nc.psum_tensor(f"bank{n}", [P, 512], f32)) for n in range(8)]
        S1, S2, PV, PJ, TR = banks[0:2], banks[2:4], banks[4], banks[5:7], banks[7]

        w_in = sem("w_in")
        w_fold = sem("w_fold")
        w_fold_out = sem("w_fold_out")
        fus_sem = sem("fus_sem")
        fus_exp = sem("fus_exp")
        wo_ready = sem("wo_ready")
        bias_ps = sem("bias_ps")
        const_pool = sem("const_pool")
        const_dve = sem("const_dve")
        zeroed = sem("zeroed")
        x_in = [sem("x_in0"), sem("x_in1")]
        xr_in = [sem("xr_in0"), sem("xr_in1")]
        ln_var = [sem(f"ln_var{n}") for n in range(5)]
        ln_rstd = [sem(f"ln_rstd{n}") for n in range(5)]
        xn_ready = sem("xn_ready")
        xnT_full = sem("xnT_full")
        xnT_ready = sem("xnT_ready")
        pj_full = sem("pj_full")
        v_full = sem("v_full")
        x32_ready = sem("x32_ready")
        hi_ready = sem("hi_ready")
        rest_ready = sem("rest_ready")
        mid_ready = sem("mid_ready")
        lo_ready = sem("lo_ready")
        spread = [sem(f"spread{n}") for n in range(4)]
        v_ready = sem("v_ready")
        s1_full = sem("s1_full")
        s1_read = sem("s1_read")
        mparts_ready = [sem("mparts_l"), sem("mparts_g")]
        mT_full = [sem("mT_full_l"), sem("mT_full_g")]
        mT_ready = [sem("mT_ready_l"), sem("mT_ready_g")]
        m_in = [sem("m_in_l"), sem("m_in_g")]
        s2_full = sem("s2_full")
        p_ready = sem("p_ready")
        pv_full = sem("pv_full")
        ot_ready = sem("ot_ready")
        nrm_full = [sem("nrm_full_l"), sem("nrm_full_g")]
        on_ready = [sem("on_ready_l"), sem("on_ready_g")]
        onT_full = [sem("onT_full_l"), sem("onT_full_g")]
        onT_ready = [sem("onT_ready_l"), sem("onT_ready_g")]
        o_full = sem("o_full")
        f_ready = sem("f_ready")
        n1_ready = sem("n1_ready")
        y_ready = sem("y_ready")
        z_ready = sem("z_ready")
        x1_ready = sem("x1_ready")
        o_norm = sem("o_norm")
        o_ready = sem("o_ready")
        o_out = sem("o_out")
        xn2_ready = sem("xn2_ready")
        x2T_full = sem("x2T_full")
        x2T_ready = sem("x2T_ready")
        lg_full = sem("lg_full")
        lg_ready = sem("lg_ready")
        hot_ready = sem("hot_ready")
        gsum_ready = sem("gsum_ready")
        cs_full = sem("cs_full")
        cs_read = sem("cs_read")
        slot_ready = sem("slot_ready")
        scat = sem("scat")

        gu_in = [sem(f"gu_in{n}") for n in range(3)]
        down_in = [sem(f"down_in{n}") for n in range(3)]
        er_in = [sem(f"er_in{n}") for n in range(RING)]
        xe_ready = sem("xe_ready")
        eT_full = sem("eT_full")
        eT_ready = sem("eT_ready")
        gu_full = sem("gu_full")
        sg_ready = sem("sg_ready")
        h_ready = sem("h_ready")
        ye_full = sem("ye_full")
        ze_ready = sem("ze_ready")
        ve_ready = sem("ve_ready")
        rs_ready = sem("rs_ready")
        ne_ready = sem("ne_ready")
        oe_ready = sem("oe_ready")
        oe_out = [sem(f"oe_out{n}") for n in range(RING)]

        TR_USES = [("x2T", 3, x2T_ready, 1, 0), ("lg", 3, lg_ready, 1, 0), ("n_g0", 2, on_ready[1], 2, 0),
                   ("n_g1", 2, on_ready[1], 2, 1), ("mT_g", 1, mT_ready[1], 1, 0), ("oT_g", 2, onT_ready[1], 1, 0),
                   ("cs", 3, cs_read, 1, 0), ("op", 2, f_ready, 1, 0), ("n_l0", 1, on_ready[0], 2, 0),
                   ("n_l1", 1, on_ready[0], 2, 1), ("mT_l", 0, mT_ready[0], 1, 0), ("oT_l", 1, onT_ready[0], 1, 0)]
        PJ_USES = [("xnT", 0, xnT_ready, 1, 0), ("p0", 0, x32_ready, 4, 0), ("p1", 0, x32_ready, 4, 1),
                   ("p2", 0, x32_ready, 4, 2), ("p3", 0, x32_ready, 4, 3), ("v0", 0, v_ready, 2, 0),
                   ("v1", 0, v_ready, 2, 1)]
        AT = {"xnT": 0, "x2T": 0, "split_g": 0, "p0": 1, "lg": 1, "p1": 2, "top": 2, "p2": 3, "n_g0": 3, "p3": 4,
              "n_g1": 4, "norm0": 4, "v0": 5, "mT_g": 5, "gate": 5, "v1": 6, "oT_g": 6, "cs": 7, "op": 8, "split_l": 10,
              "f1": 10, "n_l0": 11, "n_l1": 12, "stats_y": 12, "mT_l": 13, "oT_l": 14, "z": 14, "stats_x1": 17, "xn2": 20,
              "stats_xn2": 22, "o_norm": 1}
        GROUP_AT = {3: 0, 5: 1, 7: 2, 9: 3, 13: 4, 17: 5, 21: 6}
        LAST_GROUP_AT = 1
        S1_AT = {6: (0, 1), 7: (2, 3), 8: (4, 5), 9: (6, 7), 10: (8, 9), 11: (10, 11), **{k: (k,) for k in range(12, 24)}}

        def wait_alone(eng, sem, value):
            if not isinstance(value, int):
                value = eng.to_reg(value)
            eng.wait_ge(const_pool, 1)
            eng.wait_ge(sem, value)

        def wait_read(eng, uses, name, s, ago):
            at = [u[0] for u in uses].index(name)
            step, left = s, ago
            while left:
                at -= 1
                if at < 0:
                    at, step = len(uses) - 1, back(step)
                    if step[0] is None and step[1] < 0:
                        return
                w = back(step, uses[at][1])
                left -= exists(w)
            eng.wait_ge(uses[at][2], nth(w, uses[at][3], uses[at][4]))

        def pj_bank(name, par):
            return PJ[([u[0] for u in PJ_USES].index(name) + par) % 2]

        def steps(eng, one):
            for s in range(4):
                one((None, s), s % 2)
            with eng.Fori(0, (NW - 6) // 2) as i:
                one((i, 4), 0)
                one((i, 5), 1)
            for s in range(NW - 2, NW + 3):
                one((None, s), s % 2)

        def expert_turns(eng, one, tail=0):
            turns = (E - RING) // RING
            for e in range(RING):
                one((None, e))
            with eng.Fori(0, turns) as i:
                for n in range(RING):
                    one((i, RING + n))
            for e in range(RING * (turns + 1), E + tail):
                one((None, e))

        def eexists(e):
            return e[0] is not None or 0 <= e[1] < E

        def eth(e, per=1, k=0):
            i, n = e
            n = n * per + k + 1
            return n if i is None else i * (RING * per) + n

        def ering(e, size, per):
            i, n = e
            n = per * (n // size + 1)
            return n if i is None else i * (RING // size * per) + n

        def enum(e):
            return e[1] if e[0] is None else e[0] * RING + e[1]

        def alternate(w, per):
            i, n = w
            n = per * (n // 2 + 1)
            return n if i is None else i * per + n

        def stages(s):
            return [w if exists(w) else None for w in (s, back(s, 1), back(s, 2), back(s, 3))]

        def q_stack(par, b, h, lo, n, rows=KROWS):
            return stack[0:rows, par, b, 0, h % 8, h // 8, lo:lo + n]

        def k_stack(par, b, h, lo, n, rows=KROWS):
            return stack[0:rows, par, b, 1, h % 8, h // 8, lo:lo + n]

        block = ctx.enter_context(nc.Block())

        @block.sync
        def _(sp):
            for b, (p_, w_, o_, k_, v_, c_) in enumerate(((pT_l, winT_l, woT_l, bqk_l, bv_l, bo_l),
                                                          (pT_g, winT_g, woT_g, bqk_g, bv_g, bo_g))):
                sp.dma_start(pT[:, b, :, :], p_.rearrange("(c p) n -> p c n", p=P)).then_inc(w_in, 16)
                sp.dma_start(winT[:, b, :, :], w_.rearrange("(c p) n -> p c n", p=P)).then_inc(w_in, 16)
                sp.dma_start(wo[:, 2 * b:2 * b + 2, :], o_.rearrange("(c p) n -> p c n", p=P)).then_inc(w_in, 16)
                sp.dma_start(bqk[:, b, :], k_).then_inc(w_in, 16)
                sp.dma_start(bv[:, 2 * b:2 * b + 2], v_).then_inc(w_in, 16)
                sp.dma_start(bo[:, b, :], c_.partition_broadcast(P)).then_inc(w_in, 16)
            sp.dma_start(fus[:, :], fusion_w.partition_broadcast(P)).then_inc(w_in, 16)
            sp.dma_start(gamma_row[:, :], gamma.partition_broadcast(P)).then_inc(w_in, 16)
            sp.dma_start(beta_row[:, :], beta.partition_broadcast(P)).then_inc(w_in, 16)
            sp.dma_start(wr[:, :, :], w_router.rearrange("(c p) n -> p c n", p=P)).then_inc(w_in, 16)
            for w in range(2):
                sp.dma_start(xw[:, w, :, :], x_w[w]).then_inc(x_in[w], 16)
            sp.wait_ge(w_fold, 8)
            sp.wait_ge(const_dve, 1)

            def zero_slots(n):
                dst = slots_d.rearrange("(p g) f -> p g f", p=P)[:, n * ZREP:min((n + 1) * ZREP, NSLOT // P), :]
                sp.dma_start(dst, zeros[:, :].unsqueeze(1).to_broadcast(list(dst.shape))).then_inc(zeroed, 16)

            def expert_weights(e):
                r, before = e[1] % 3, (e[0], e[1] - 3)
                if eexists(before):
                    wait_alone(sp, gu_full, eth(before, 2, 1))
                for n in range(3):
                    if n == 2 and eexists(before):
                        wait_alone(sp, ye_full, eth(before))
                    sp.dma_start(ew[:, r, n, :, :], w_e[n][bass.ds(enum(e), 1)].rearrange("e p c f -> (e p) c f")
                                 ).then_inc((gu_in, gu_in, down_in)[n][r], 16)

            w_e = [w.rearrange("e (c p) f -> e p c f", p=P) for w in (w_gate, w_up, w_down)]

            def spread_parts(j, a, par):
                b, qk = j // 2, j % 2
                wait_alone(sp, lo_ready, nth(a, 4, j))
                for n, part in enumerate((E_PARTS_Q, E_PARTS_K)[qk]):
                    sp.dma_start(stack[HD * n:HD * n + HD, par, b, qk, :, :, :].rearrange("d h t n -> d h (t n)"),
                                 parts[:, j, part, :]).then_inc(spread[j], 16)

            def maxima_in(b, w, par):
                wait_alone(sp, mT_ready[b], nth(w, 1))
                sp.dma_start(stack[NPART:KROWS, par, b, 0, :, :, :].rearrange("r h t n -> r (h t) n"), mT[:, b, :]
                             ).then_inc(m_in[b], 16)

            def step(s, par):
                a, c, d, f = stages(s)
                ahead = back(s, -2)
                if a and (ahead[0] is not None or ahead[1] < NW):
                    wait_alone(sp, xn_ready, nth(a, 1))
                    sp.dma_start(xw[:, par, :, :], x_w[bass.ds(num(ahead), 1)].rearrange("w p q f -> (w p) q f")
                                 ).then_inc(x_in[par], 16)
                if a:
                    if exists(back(a, 2)):
                        wait_alone(sp, s2_full, nth(back(a, 2), UNITS, UNITS - 1))
                    spread_parts(0, a, par)
                    spread_parts(1, a, par)
                if c:
                    maxima_in(1, c, 1 - par)
                if a:
                    spread_parts(2, a, par)
                    spread_parts(3, a, par)
                if d:
                    if exists(back(d, 2)):
                        wait_alone(sp, x1_ready, nth(back(d, 2), 1))
                    sp.dma_start(xr[:, par, :, :], x_w[bass.ds(num(d), 1)].rearrange("w p q f -> (w p) q f")
                                 ).then_inc(xr_in[par], 16)
                if f:
                    wait_alone(sp, o_ready, nth(f, 1))
                    sp.dma_start(out_w[bass.ds(num(f), 1)].rearrange("w p q f -> (w p) q f"), obuf[:, :, :]).then_inc(o_out, 16)
                if a:
                    maxima_in(0, a, par)
                if s[0] is None and s[1] < 3:
                    for n in range(s[1], ZDMAS, 3):
                        zero_slots(n)
                if s[0] is None and s[1] == NW - 2:
                    for e in range(3):
                        expert_weights((None, e))

            steps(sp, step)

            sp.wait_ge(pv_full, GROUPS * NW)
            sp.wait_ge(scat, 32 * NW)
            rows_e = slots_d.rearrange("(e r) f -> e r f", e=E)

            def expert(e):
                r, before = e[1] % RING, (e[0], e[1] - RING)
                if eexists(before):
                    wait_alone(sp, oe_ready, eth(before))
                for n, (lo, m) in enumerate(CHUNKS):
                    sp.dma_start(erows[0:m, r, n, :], rows_e[bass.ds(enum(e), 1), lo:lo + m, :].rearrange("e r f -> (e r) f")
                                 ).then_inc(er_in[r], 16)
                if e[0] is not None or e[1] >= 3:
                    expert_weights(e)

            expert_turns(sp, expert)
            sp.wait_ge(o_out, 16 * NW)
            for r in range(RING):
                sp.wait_ge(oe_out[r], 16 * NCH * len(range(r, E, RING)))

        @block.gpsimd
        def _(pool):
            pool.memset(ident[:, :], 0.0)
            pool.memset(identb[:, :], 0.0)
            pool.memset(tri[:, :], 1.0)
            pool.memset(earlier[:, :], 1.0)
            pool.memset(onesb[:, :], 1.0)
            pool.memset(mhalf[:, :], -0.5)
            pool.iota(left[:, :], pattern=[[-P, 2]], base=T, channel_multiplier=-1, allow_small_or_imprecise_dtypes=True)
            pool.iota(iota_e[:, :], pattern=[[1, E]], base=0, channel_multiplier=0, allow_small_or_imprecise_dtypes=True)
            pool.drain()
            for m in (ident, identb):
                pool.affine_select(out=m[:, :], in_=m[:, :], compare_op=ALU.not_equal, fill=1.0,
                                   base=0, pattern=[[-1, P]], channel_multiplier=1)
            pool.affine_select(out=tri[:, :], in_=tri[:, :], compare_op=ALU.is_gt, fill=0.0,
                               base=0, pattern=[[-1, P]], channel_multiplier=1)
            pool.affine_select(out=earlier[:, :], in_=earlier[:, :], compare_op=ALU.is_gt, fill=0.0,
                               base=0, pattern=[[1, P]], channel_multiplier=-1)
            pool.drain().then_inc(const_pool, 1)

            def inv_std(n, w):
                wait(pool, ln_var[n], w)
                pool.tensor_tensor(rstd[:, n, :], ve[:, n, :], mhalf[:, 0:2], ALU.pow).then_inc(ln_rstd[n], 1)

            def remainder(j, a):
                wait(pool, hi_ready, a, 4, j)
                if j < 2:
                    wait(pool, mid_ready, back(a), 4, j + 2)
                else:
                    wait(pool, mid_ready, a, 4, j - 2)
                pool.tensor_tensor(rest[:, j % 2, :], x32[:, j % 2, :], parts[:, j, 0, :], ALU.subtract
                                   ).then_inc(rest_ready, 1)

            def low_part(j, a):
                wait(pool, mid_ready, a, 4, j)
                pool.tensor_tensor(parts[:, j, 2, :], rest[:, j % 2, :], parts[:, j, 1, :], ALU.subtract
                                   ).then_inc(lo_ready, 1)

            def step(s, par):
                a, c, d, f = stages(s)
                nxt = back(s, -1)
                if a:
                    for j in range(4):
                        remainder(j, a)
                        if j == 3 and (nxt[0] is not None or nxt[1] < NW):
                            inv_std(0, nxt)
                        low_part(j, a)
                if f:
                    wait(pool, o_norm, f)
                    pool.tensor_tensor(obuf[:, :, :], obuf[:, :, :], x1[:, :, :], ALU.add).then_inc(o_ready, 1)
                    pool.wait_ge(zeroed, 16 * ZDMAS)
                    wait_alone(pool, slot_ready, nth(f, 1))
                    for q in range(2):
                        pool.indirect_dma_start(
                            out=slots_d, out_offset=bass.IndirectOffsetOnAxis(ap=slot_u[:, q:q + 1], axis=0),
                            in_=xrow[:, q, :], in_offset=None, bounds_check=NSLOT - 1, oob_is_err=False).then_inc(scat, 16)
                if d:
                    inv_std(1, d)
                    wait(pool, n1_ready, d)
                    pool.tensor_tensor(ybuf[:, :, :], fbuf[:, :, :], gamma_row[:, :].unsqueeze(1).to_broadcast([P, 2, D]), ALU.mult)
                    pool.drain()
                    pool.tensor_tensor(ybuf[:, :, :], ybuf[:, :, :], beta_row[:, :].unsqueeze(1).to_broadcast([P, 2, D]), ALU.add
                                       ).then_inc(y_ready, 1)
                    inv_std(2, d)
                    wait(pool, z_ready, d)
                    if exists(back(d)):
                        pool.wait_ge(scat, nth(back(d), 32, 31))
                    wait(pool, xn2_ready, back(d))
                    pool.wait_ge(xr_in[par], xr_count(d))
                    pool.tensor_tensor(x1[:, :, :], ybuf[:, :, :], xr[:, par, :, :], ALU.add).then_inc(x1_ready, 1)
                    inv_std(3, d)
                    inv_std(4, d)

            def xr_count(d):
                i, n = d
                n = 16 * (n // 2 + 1)
                return n if i is None else i * 16 + n

            pool.wait_ge(const_dve, 2)
            for p_ in range(2):
                for qk, base0, step_a in ((0, 7, -4), (1, 3, 4)):
                    rows = stack[NPART:BROW, p_, 1, qk, :, :, :].rearrange("r h t (a n) -> r (h t) a n", a=2)
                    last = pool.affine_select(out=rows, in_=rows, compare_op=ALU.not_equal, fill=0.0, base=base0,
                                              pattern=[[0, NH], [step_a, 2], [0, P]], channel_multiplier=-1)
            pool.drain().then_inc(const_pool, 1)
            inv_std(0, (None, 0))
            steps(pool, step)

            pool.wait_ge(o_out, 16 * NW)

            def expert(e):
                last, old = back(e), back(e, 2)
                if eexists(old):
                    r = old[1] % RING
                    pool.wait_ge(ne_ready, eth(old))
                    for lo, n, m in PIECES:
                        done = pool.tensor_tensor(zb[0:m, r, lo:lo + n, :], zb[0:m, r, lo:lo + n, :],
                                                  erows[0:m, r, lo:lo + n, 0:D], ALU.add)
                    done.then_inc(oe_ready, 1)
                    wait_alone(pool, oe_ready, eth(old))
                    for n, (lo, m) in enumerate(CHUNKS):
                        pool.indirect_dma_start(
                            out=out_t, out_offset=bass.IndirectOffsetOnAxis(ap=idx_e[0:m, r, n:n + 1], axis=0),
                            in_=zb[0:m, r, n, :], in_offset=None, bounds_check=T - 1, oob_is_err=False).then_inc(oe_out[r], 16)
                if eexists(last):
                    pool.wait_ge(ve_ready, eth(last))
                    pool.tensor_tensor(rs_e[:, last[1] % 2, :], ve_e[:, last[1] % 2, :], mhalf[:, 0:NCH], ALU.pow
                                       ).then_inc(rs_ready, 1)

            expert_turns(pool, expert, tail=2)

        @block.scalar
        def _(act):
            act.wait_ge(fus_sem, 1)
            act.activation(fus_e[:, :], fus[:, :], ACT.Exp, bias=fus_m[:, 0:1]).then_inc(fus_exp, 1)
            n = 0
            for b in range(2):
                for c in range(2):
                    act.wait_ge(w_fold, n + 1)
                    act.activation(weff[:, b, c, 0:512].rearrange("p (x d h) -> p x d h", d=HD, h=8),
                                   banks[2 * (n // 2 % 2)][:, :].rearrange("p (x h d) -> p x d h", d=HD, h=8), ACT.Copy)
                    act.wait_ge(w_fold, n + 2)
                    act.activation(weff[:, b, c, 512:768], banks[2 * (n // 2 % 2) + 1][:, 0:256], ACT.Copy).then_inc(w_fold_out, 1)
                    n += 2

            def exps(u, c):
                wait(act, s2_full, c, UNITS, u)
                if u < 8:
                    wait(act, pv_full, back(c), GROUPS, 6 + u // 4)
                elif u < 16:
                    wait(act, pv_full, c, GROUPS, (u - 8) // 2)
                else:
                    wait(act, pv_full, c, GROUPS, 4 + (u - 16) // 4)
                act.activation(pt[:, u % 8, :], S2[u % 2][:, :], ACT.Exp).then_inc(p_ready, 1)

            def values_out(g, c):
                wait(act, pv_full, c, GROUPS, g)
                b = g // 4
                wait(act, nrm_full[b], back(c), 2, 1)
                act.activation(OT[:, b, g % 4, :], PV[:, 0:WIN], ACT.Copy).then_inc(ot_ready, 1)

            def projected(j, a, par):
                wait(act, pj_full, a, 4, j)
                wait(act, rest_ready, a if j >= 2 else back(a), 4, (j - 2) % 4)
                b, qk = j // 2, j % 2
                bank = pj_bank(f"p{j}", par)
                for t in range(2):
                    last = act.activation(x32[:, j % 2, t * WIN:(t + 1) * WIN], bank[:, t * WIN:(t + 1) * WIN], ACT.Identity,
                                          bias=bqk[:, b, 2 * qk + t:2 * qk + t + 1], scale=QSCALE if qk == 0 else 1.0)
                last.then_inc(x32_ready, 1)

            def v_out(q, a, par):
                wait(act, v_full, a, 2, q)
                wait(act, pv_full, back(a, 2), GROUPS, GROUPS - 1)
                act.activation(v_pad[:, par, q, :, :, 0:HD],
                               pj_bank(f"v{q}", par)[:, :].rearrange("p (b h d) -> p b h d", b=2, d=HD), ACT.Copy
                               ).then_inc(v_ready, 1)

            def maxima_out(b, a):
                wait(act, mT_full[b], a)
                if exists(back(a)):
                    act.wait_ge(m_in[b], nth(back(a), 16, 15))
                act.activation(mT[:, b, :], TR[0:48, 0:WIN // 2].bitcast(bf16), ACT.Copy).then_inc(mT_ready[b], 1)

            def onT_out(b, w):
                wait(act, onT_full[b], w)
                wait(act, o_full, back(w))
                act.activation(OnT[:, b, :, :].rearrange("p t n -> p (t n)"), TR[:, :], ACT.Copy).then_inc(onT_ready[b], 1)

            def step(s, par):
                a, c, d, f = stages(s)
                for k in range(UNITS):
                    if c:
                        exps(k, c)
                        if k in GROUP_AT:
                            values_out(GROUP_AT[k], c)
                    if d and k == LAST_GROUP_AT:
                        values_out(GROUPS - 1, d)
                    if a and k == AT["xnT"]:
                        wait(act, xnT_full, a)
                        wait(act, v_full, back(a), 2, 1)
                        act.activation(xnT[:, :, :].rearrange("p c n -> p (c n)"), pj_bank("xnT", par)[:, :], ACT.Copy
                                       ).then_inc(xnT_ready, 1)
                    if f and k == AT["x2T"]:
                        wait(act, x2T_full, f)
                        act.activation(xn2T[:, :, :].rearrange("p c n -> p (c n)"), TR[:, :], ACT.Copy).then_inc(x2T_ready, 1)
                    for j in range(4):
                        if a and k == AT[f"p{j}"]:
                            projected(j, a, par)
                    if c and k == AT["mT_g"]:
                        maxima_out(1, c)
                    for q in range(2):
                        if a and k == AT[f"v{q}"]:
                            v_out(q, a, par)
                    if d and k == AT["oT_g"]:
                        onT_out(1, d)
                    if f and k == AT["gate"]:
                        wait(act, lg_ready, f)
                        for q in range(2):
                            last = act.activation(egate[:, q, :], lg[:, q, :], ACT.Exp, bias=ntop[:, q:q + 1],
                                                  accum_out=gsum[:, q:q + 1])
                        last.then_inc(gsum_ready, 1)
                    if a and k == AT["mT_l"]:
                        maxima_out(0, a)
                    if c and k == AT["oT_l"]:
                        onT_out(0, c)

            steps(act, step)

            def transposed(e):
                act.wait_ge(eT_full, eth(e))
                for c in range(2):
                    last = act.activation(eT[:, e[1] % 2, c, :], banks[c][:, 0:CAP], ACT.Copy)
                last.then_inc(eT_ready, 1)

            def expert(e):
                for m in range(2):
                    act.wait_ge(gu_full, eth(e, 2, m))
                    if eexists(back(e)):
                        act.wait_ge(h_ready, eth(back(e), 2, m))
                    act.activation(sg[:, m, :], banks[2 + 2 * m][:, 0:CAP], ACT.Silu).then_inc(sg_ready, 1)
                if eexists(back(e, -1)):
                    transposed(back(e, -1))

            transposed((None, 0))
            expert_turns(act, expert)

        @block.vector
        def _(dve):
            dve.memset(zeros[:, :], 0.0)
            dve.memset(base[:, :], 0.0)
            dve.memset(mv_e[:, :, :, :], 0.0)
            dve.memset(v_pad[:, :, :, :, :, :], 0.0)
            dve.drain()
            for p_ in range(2):
                for q in range(2):
                    for b in range(2):
                        dve.memset(v_pad[:, p_, q, b, :, HD:HD + 1], 1.0)
            dve.drain().then_inc(const_dve, 1)
            dve.wait_ge(w_in, 16 * 16)
            dve.tensor_copy(bvb[:, :, :], bv[:, :].unsqueeze(2).to_broadcast([P, 4, P]))
            dve.reduce_max(fus_m[:, 1:2], fus[:, :], AX.X)
            dve.tensor_scalar(bqk[:, :, 0:2], bqk[:, :, 0:2], QSCALE, None, ALU.mult)
            dve.drain()
            dve.tensor_scalar(fus_m[:, 0:1], fus_m[:, 1:2], -1.0, None, ALU.mult).then_inc(fus_sem, 1)
            dve.wait_ge(fus_exp, 1)
            dve.reduce_sum(fus_m[:, 1:2], fus_e[:, :], AX.X)
            dve.drain()
            dve.reciprocal(fus_m[:, 1:2], fus_m[:, 1:2])
            dve.drain()
            dve.tensor_scalar(fus_e[:, :], fus_e[:, :], fus_m[:, 1:2], None, ALU.mult)
            dve.drain()
            for b in range(2):
                dve.tensor_scalar(wo[:, 2 * b:2 * b + 2, :], wo[:, 2 * b:2 * b + 2, :], fus_e[:, b:b + 1], None, ALU.mult)
                dve.tensor_scalar(bo[:, b, :], bo[:, b, :], fus_e[:, b:b + 1], None, ALU.mult)
            dve.drain()
            dve.tensor_tensor(bias_row[:, :], bo[:, 0, :], bo[:, 1, :], ALU.add).then_inc(wo_ready, 1)
            dve.wait_ge(bias_ps, 1)
            dve.drain()
            dve.tensor_tensor(bias_row[:, :], TR[:, 0:D], bias_row[:, :], ALU.add)
            dve.wait_ge(w_fold, 8)
            for p_ in range(2):
                for b in range(2):
                    dve.memset(stack[NPART:BROW, p_, b, :, :, :, :].rearrange("r x h t n -> r (x h t n)"), 1.0)
            dve.drain().then_inc(const_dve, 1)

            def stats(n, src, w):
                for q in range(2):
                    dve.bn_stats(bst[:, n, q, :], src[:, q, :])
                dve.drain()
                for q in range(2):
                    dve.bn_aggr(mv[:, n, q, :], bst[:, n, q, :])
                dve.drain()
                dve.tensor_scalar(ve[:, n, :], mv[:, n, :, 1], EPS, None, ALU.add).then_inc(ln_var[n], 1)

            def norm(n, dst, src, sem, w):
                wait(dve, ln_rstd[n], w)
                for q in range(2):
                    last = dve.tensor_scalar(dst[:, q, :], src[:, q, :], mv[:, n, q, 0:1], rstd[:, n, q:q + 1],
                                             ALU.subtract, ALU.mult)
                last.then_inc(sem, 1)

            def first_stats(w, par):
                dve.wait_ge(x_in[par], alternate(w, 16))
                stats(0, xw[:, par, :, :], w)

            def first_norm(w, par):
                wait(dve, xnT_full, back(w))
                norm(0, xn, xw[:, par, :, :], xn_ready, w)

            def high_part(j, a):
                wait(dve, x32_ready, a, 4, j)
                if exists(back(a)):
                    dve.wait_ge(spread[j], nth(back(a), 96, 95))
                dve.tensor_copy(parts[:, j, 0, :], x32[:, j % 2, :]).then_inc(hi_ready, 1)

            def mid_part(j, a):
                wait(dve, rest_ready, a, 4, j)
                dve.tensor_copy(parts[:, j, 1, :], rest[:, j % 2, :]).then_inc(mid_ready, 1)

            def maximum(u, a):
                wait(dve, s1_full, a, UNITS, u)
                if u < LU:
                    dst = mx[:, 0, :, :].rearrange("p q (h t) -> p t h q", t=2)[:, u // 4, (2 * u) % 8:(2 * u) % 8 + 2, :]
                    src = S1[u % 2][:, :].rearrange("p (h q n) -> p h q n", h=2, q=2)
                else:
                    h = u - LU
                    dst = mx[:, 1, :, 2 * (h % 8) + h // 8]
                    src = S1[u % 2][:, :].rearrange("p (q n) -> p q n", q=2)
                dve.reduce_max(dst, src, AX.X).then_inc(s1_read, 1)

            def split_maxima(b, a):
                dve.drain()
                wait(dve, mT_full[b], back(a))
                dve.tensor_scalar(mparts[:, b, :, 0, :], mx[:, b, :, :], -1.0, None, ALU.mult)
                dve.drain()
                dve.scalar_tensor_tensor(mneg[:, b, :, :], mx[:, b, :, :], -1.0, mparts[:, b, :, 0, :], ALU.mult, ALU.subtract)
                dve.drain()
                dve.tensor_copy(mparts[:, b, :, 1, :], mneg[:, b, :, :])
                dve.drain()
                dve.tensor_tensor(mparts[:, b, :, 2, :], mneg[:, b, :, :], mparts[:, b, :, 1, :], ALU.subtract
                                  ).then_inc(mparts_ready[b], 1)

            def normalise(b, q, w):
                wait(dve, nrm_full[b], w, 2, q)
                src = TR[:, :].rearrange("p (h m) -> p h m", m=32)
                dve.reciprocal(rden[:, b, :], src[:, :, HD])
                dve.drain()
                wait(dve, onT_full[b], back(w))
                dve.tensor_tensor(On[:, b, q, :].rearrange("p (h d) -> p h d", d=HD), src[:, :, 0:HD],
                                  rden[:, b, :].unsqueeze(2).to_broadcast([P, NH, HD]), ALU.mult).then_inc(on_ready[b], 1)

            def route_top(d):
                wait(dve, lg_full, d)
                wait(dve, gsum_ready, back(d))
                dve.tensor_copy(lg[:, :, :], TR[:, 0:2 * E].rearrange("p (q e) -> p q e", q=2))
                dve.drain()
                for q in range(2):
                    dve.max(top[:, q, :], lg[:, q, :])
                dve.drain()
                dve.tensor_scalar(ntop[:, :], top[:, :, 0], -1.0, None, ALU.mult).then_inc(lg_ready, 1)
                for q in range(2):
                    dve.max_index(top_i[:, q, :], top[:, q, :], lg[:, q, :])
                dve.drain()
                dve.tensor_copy(idx_f[:, :], top_i[:, :, 0])
                dve.drain()
                wait(dve, cs_full, back(d))
                for q in range(2):
                    last = dve.tensor_scalar(hot[:, q, :], iota_e[:, :], idx_f[:, q:q + 1], None, ALU.is_equal)
                last.then_inc(hot_ready, 1)

            def route_slot(d):
                wait(dve, cs_full, d)
                dve.tensor_tensor(pos[:, :, :], TR[:, 0:2 * E].rearrange("p (q e) -> p q e", q=2),
                                  base[:, :].unsqueeze(1).to_broadcast([P, 2, E]), ALU.add)
                wait(dve, gsum_ready, d)
                dve.reciprocal(gate1[:, :], gsum[:, :])
                dve.drain()
                dve.tensor_tensor(base[:, :], TR[:, 2 * E:3 * E], base[:, :], ALU.add).then_inc(cs_read, 1)
                dve.tensor_tensor(posh[:, :, :], pos[:, :, :], hot[:, :, :], ALU.mult)
                dve.drain()
                dve.reduce_sum(pos1[:, :], posh[:, :, :], AX.X)
                dve.drain()
                dve.tensor_scalar(okf[:, :], pos1[:, :], float(CAP), None, ALU.is_lt)
                dve.scalar_tensor_tensor(slotf[:, :], idx_f[:, :], float(CAP), pos1[:, :], ALU.mult, ALU.add)
                dve.drain()
                dve.tensor_scalar(far[:, :], okf[:, :], -float(4 * NSLOT), float(4 * NSLOT), ALU.mult, ALU.add)
                dve.tensor_copy(xrow[:, :, GATE], gate1[:, :])
                dve.tensor_copy(xrow[:, :, TOKEN], left[:, :])
                dve.drain()
                if exists(back(d)):
                    dve.wait_ge(scat, nth(back(d), 32, 31))
                dve.tensor_tensor(slot_u[:, :], slotf[:, :], far[:, :], ALU.add).then_inc(slot_ready, 1)
                dve.tensor_scalar(left[:, :], left[:, :], -float(WIN), None, ALU.add)

            def step(s, par):
                a, c, d, f = stages(s)
                nxt = back(s, -1)
                first = a and (nxt[0] is not None or nxt[1] < NW)
                for k in range(UNITS):
                    if c and k == AT["split_g"]:
                        split_maxima(1, c)
                    for j in range(4):
                        if a and k == AT[f"p{j}"]:
                            high_part(j, a)
                        if a and k == AT[f"p{j}"] + 1:
                            mid_part(j, a)
                    if f and k == AT["top"]:
                        route_top(f)
                    for q in range(2):
                        if d and k == AT[f"n_g{q}"]:
                            normalise(1, q, d)
                        if c and k == AT[f"n_l{q}"]:
                            normalise(0, q, c)
                    if f and k == AT["o_norm"]:
                        if exists(back(f)):
                            dve.wait_ge(o_out, nth(back(f), 16, 15))
                        norm(4, obuf, xn2, o_norm, f)
                    if first and k == AT["norm0"]:
                        first_stats(nxt, 1 - par)
                    if first and k == AT["norm0"] + 1:
                        first_norm(nxt, 1 - par)
                    if f and k == AT["cs"]:
                        route_slot(f)
                    if a and k == AT["split_l"]:
                        split_maxima(0, a)
                    if a:
                        for u in S1_AT.get(k, ()):
                            maximum(u, a)
                    if d and k == AT["op"]:
                        wait(dve, o_full, d)
                        wait(dve, y_ready, back(d))
                        dve.tensor_tensor(fbuf[:, :, :], TR[:, :].rearrange("p (q f) -> p q f", q=2),
                                          bias_row[:, :].unsqueeze(1).to_broadcast([P, 2, D]), ALU.add).then_inc(f_ready, 1)
                        dve.drain()
                        stats(1, fbuf, d)
                    if d and k == AT["f1"]:
                        norm(1, fbuf, fbuf, n1_ready, d)
                    if d and k == AT["stats_y"]:
                        wait(dve, y_ready, d)
                        stats(2, ybuf, d)
                    if d and k == AT["z"]:
                        norm(2, ybuf, ybuf, z_ready, d)
                    if d and k == AT["stats_x1"]:
                        wait(dve, x1_ready, d)
                        stats(3, x1, d)
                    if d and k == AT["xn2"]:
                        wait(dve, x2T_full, back(d))
                        norm(3, xn2, x1, xn2_ready, d)
                        dve.tensor_copy(xrow[:, :, MEAN], mv[:, 3, :, 0])
                        dve.tensor_copy(xrow[:, :, RSTD], rstd[:, 3, :])
                    if d and k == AT["stats_xn2"]:
                        dve.drain()
                        stats(4, xn2, d)

            first_stats((None, 0), 0)
            first_norm((None, 0), 0)
            steps(dve, step)

            def norms(e):
                r = e[1] % RING
                dve.wait_ge(er_in[r], ering(e, RING, 16 * NCH))
                if eexists(back(e, RING)):
                    dve.wait_ge(oe_out[r], ering(back(e, RING), RING, 16 * NCH))
                for lo, n, m in PIECES:
                    dve.tensor_scalar(idx_e[0:m, r, lo:lo + n], erows[0:m, r, lo:lo + n, TOKEN], -1.0, float(T), ALU.mult, ALU.add)
                for n, (lo, m) in enumerate(CHUNKS):
                    last = dve.tensor_scalar(zb[0:m, r, n, :], erows[0:m, r, n, 0:D], erows[0:m, r, n, MEAN:MEAN + 1],
                                             erows[0:m, r, n, RSTD:RSTD + 1], ALU.subtract, ALU.mult)
                last.then_inc(xe_ready, 1)

            def expert(e):
                ahead, last, old = back(e, -1), back(e), back(e, 2)
                if eexists(ahead):
                    norms(ahead)
                if eexists(old):
                    r, b = old[1] % RING, old[1] % 2
                    dve.wait_ge(rs_ready, eth(old))
                    for n, (lo, m) in enumerate(CHUNKS):
                        done = dve.tensor_scalar(zb[0:m, r, n, :], zb[0:m, r, n, :], mv_e[0:m, b, n, 0:1], rs_e[0:m, b, n:n + 1],
                                                 ALU.subtract, ALU.mult)
                    done.then_inc(ne_ready, 1)
                if eexists(e):
                    for m in range(2):
                        dve.wait_ge(sg_ready, eth(e, 2, m))
                        dve.tensor_tensor(hT[:, e[1] % 2, m, :], banks[3 + 2 * m][:, 0:CAP], sg[:, m, :], ALU.mult).then_inc(h_ready, 1)
                if eexists(last):
                    r, b = last[1] % RING, last[1] % 2
                    dve.wait_ge(ye_full, eth(last))
                    for n, (lo, m) in enumerate(CHUNKS):
                        done = dve.scalar_tensor_tensor(zb[0:m, r, n, :], banks[6 + n // 2][0:m, n % 2 * D:(n % 2 + 1) * D],
                                                        erows[0:m, r, n, GATE:GATE + 1], zb[0:m, r, n, :], ALU.mult, ALU.add)
                    done.then_inc(ze_ready, 1)
                    dve.drain()
                    for n, (lo, m) in enumerate(CHUNKS):
                        dve.bn_stats(bst_e[0:m, n, :], zb[0:m, r, n, :])
                    dve.drain()
                    for n, (lo, m) in enumerate(CHUNKS):
                        dve.bn_aggr(mv_e[0:m, b, n, :], bst_e[0:m, n, :])
                    dve.drain()
                    dve.tensor_scalar(ve_e[:, b, :], mv_e[:, b, :, 1], EPS, None, ALU.add).then_inc(ve_ready, 1)

            norms((None, 0))
            expert_turns(dve, expert, tail=2)

        @block.tensor
        def _(pe):
            pe.wait_ge(w_in, 16 * 16)
            n = 0
            for b in range(2):
                for c in range(2):
                    if n >= 4:
                        pe.wait_ge(w_fold_out, n // 2 - 1)
                    for half, (lo, width) in enumerate(((0, 512), (512, 256))):
                        for kc in range(2):
                            last = pe.matmul(banks[2 * (n // 2 % 2) + half][:, 0:width], pT[:, b, kc, c * P:(c + 1) * P],
                                             winT[:, b, kc, lo:lo + width], start=(kc == 0), stop=(kc == 1))
                        last.then_inc(w_fold, 1)
                    n += 2
            pe.wait_ge(wo_ready, 1)
            for c in range(4):
                last = pe.matmul(TR[:, 0:D], bvb[:, c, :], wo[:, c, :], start=(c == 0), stop=(c == 3))
            last.then_inc(bias_ps, 1)
            pe.wait_ge(const_pool, 2)
            pe.wait_ge(w_fold_out, 4)
            pe.wait_ge(const_dve, 2)

            def scores(u, c, par):
                if u == 0:
                    for j in (0, 1):
                        pe.wait_ge(spread[j], nth(c, 96, 95))
                    pe.wait_ge(m_in[0], nth(c, 16, 15))
                if u == LU:
                    for j in (2, 3):
                        pe.wait_ge(spread[j], nth(c, 96, 95))
                    pe.wait_ge(m_in[1], nth(c, 16, 15))
                if u >= 2:
                    wait(pe, p_ready, c, UNITS, u - 2)
                else:
                    wait(pe, p_ready, back(c), UNITS, UNITS - 2 + u)
                bank = S2[u % 2]
                if u < LU:
                    pe.matmul(bank[:, :], identb[:, :], tri[:, :].unsqueeze(1).to_broadcast([P, 4, P]), start=True, stop=False)
                    for h2 in range(2):
                        for j in range(2):
                            h = 2 * u + h2
                            last = pe.matmul(bank[:, (2 * h2 + j) * P:(2 * h2 + j + 1) * P], k_stack(par, 0, h, j * P, P),
                                             q_stack(par, 0, h, j * P, P), start=False, stop=(h2 == 1 and j == 1))
                else:
                    diagonal = bank[:, :].rearrange("p (a n) -> p a n", n=P)[:, 0:4:3, :]
                    pe.matmul(diagonal, identb[:, :], tri[:, :].unsqueeze(1).to_broadcast([P, 2, P]), start=True, stop=False)
                    for kb in range(2):
                        for qb in range(2):
                            last = pe.matmul(bank[:, (2 * kb + qb) * P:(2 * kb + qb + 1) * P],
                                             k_stack(par, 1, u - LU, kb * P, P, BROW), q_stack(par, 1, u - LU, qb * P, P, BROW),
                                             start=False, stop=(kb == 1 and qb == 1))
                last.then_inc(s2_full, 1)

            def values(g, c, par):
                wait(pe, ot_ready, c if g else back(c), GROUPS, (g - 1) % GROUPS)
                if g < 4:
                    wait(pe, p_ready, c, UNITS, 2 * g + 1)
                    for j in range(2):
                        for h4 in range(4):
                            last = pe.matmul(PV[32 * h4:32 * h4 + 32, j * P:(j + 1) * P], v_pad[:, par, j, 0, 4 * g + h4, :],
                                             pt[:, (2 * g + h4 // 2) % 8, (2 * (h4 % 2) + j) * P:(2 * (h4 % 2) + j + 1) * P],
                                             start=True, stop=True)
                else:
                    u0 = LU + 4 * (g - 4)
                    wait(pe, p_ready, c, UNITS, u0 + 3)
                    for kb in range(2):
                        for h4 in range(4):
                            last = pe.matmul(PV[32 * h4:32 * h4 + 32, 0:WIN], v_pad[:, par, kb, 1, 4 * (g - 4) + h4, :],
                                             pt[:, (u0 + h4) % 8, kb * WIN:(kb + 1) * WIN], start=(kb == 0), stop=(kb == 1))
                last.then_inc(pv_full, 1)

            def project(j, a, s, par):
                wait_read(pe, PJ_USES, f"p{j}", s, 2)
                bank, b, qk = pj_bank(f"p{j}", par), j // 2, j % 2
                for t in range(2):
                    for c in range(2):
                        last = pe.matmul(bank[:, t * WIN:(t + 1) * WIN], weff[:, b, c, qk * D + t * P:qk * D + (t + 1) * P],
                                         xnT[:, c, :], start=(c == 0), stop=(c == 1))
                last.then_inc(pj_full, 1)

            def project_v(q, a, s, par):
                wait_read(pe, PJ_USES, f"v{q}", s, 2)
                for c in range(2):
                    last = pe.matmul(pj_bank(f"v{q}", par)[:, :], xnT[:, c, q * P:(q + 1) * P], weff[:, :, c, 2 * D:3 * D],
                                     start=(c == 0), stop=(c == 1))
                last.then_inc(v_full, 1)

            def row_scores(u, a, par):
                if u == 0:
                    for j in (0, 1):
                        pe.wait_ge(spread[j], nth(a, 96, 95))
                if u == LU:
                    for j in (2, 3):
                        pe.wait_ge(spread[j], nth(a, 96, 95))
                if u >= 2:
                    wait(pe, s1_read, a, UNITS, u - 2)
                else:
                    wait(pe, s1_read, back(a), UNITS, UNITS - 2 + u)
                bank = S1[u % 2]
                for n in range(2):
                    for j in range(2):
                        if u < LU:
                            last = pe.matmul(bank[:, (2 * n + j) * P:(2 * n + j + 1) * P], q_stack(par, 0, 2 * u + n, j * P, P, NPART),
                                             k_stack(par, 0, 2 * u + n, j * P, P, NPART), start=True, stop=True)
                        elif j == 0:
                            last = pe.matmul(bank[:, n * WIN:(n + 1) * WIN], q_stack(par, 1, u - LU, n * P, P, NPART),
                                             k_stack(par, 1, u - LU, 0, WIN, NPART), start=True, stop=True)
                last.then_inc(s1_full, 1)

            def four_transposes(src, sem_full):
                for n in range(4):
                    last = pe.transpose(TR[:, n * P:(n + 1) * P], src(n), ident[:, :])
                last.then_inc(sem_full, 1)

            def maxima_T(b, a, s):
                pe.wait_ge(const_pool, 1)
                wait_read(pe, TR_USES, ("mT_l", "mT_g")[b], s, 1)
                wait_alone(pe, mparts_ready[b], nth(a, 1))
                trb = TR[:, :].bitcast(bf16)
                for q in range(2):
                    last = pe.transpose(trb[0:48, q * P:(q + 1) * P], mparts[:, b, q, :, :].rearrange("p r h -> p (r h)"), identb[:, :])
                last.then_inc(mT_full[b], 1)

            def norm_T(b, q, w, s):
                wait_read(pe, TR_USES, f"n_{'lg'[b]}{q}", s, 1)
                wait(pe, ot_ready, w, GROUPS, 3 + 4 * b)
                four_transposes(lambda n: OT[:, b, n, q * P:(q + 1) * P], nrm_full[b])

            def out_T(b, w, s):
                wait_read(pe, TR_USES, f"oT_{'lg'[b]}", s, 1)
                wait(pe, on_ready[b], w, 2, 1)
                four_transposes(lambda n: On[:, b, n % 2, n // 2 * P:(n // 2 + 1) * P], onT_full[b])

            def step(s, par):
                a, c, d, f = stages(s)
                for k in range(UNITS):
                    if c:
                        scores(k, c, 1 - par)
                        if k in GROUP_AT:
                            values(GROUP_AT[k], c, 1 - par)
                    if d and k == LAST_GROUP_AT:
                        values(GROUPS - 1, d, par)
                    if a and k == AT["xnT"]:
                        wait_read(pe, PJ_USES, "xnT", s, 2)
                        wait(pe, xn_ready, a)
                        bank = pj_bank("xnT", par)
                        for n in range(4):
                            last = pe.transpose(bank[:, n * P:(n + 1) * P], xn[:, n % 2, n // 2 * P:(n // 2 + 1) * P], ident[:, :])
                        last.then_inc(xnT_full, 1)
                    if f and k == AT["x2T"]:
                        wait_read(pe, TR_USES, "x2T", s, 1)
                        wait(pe, xn2_ready, f)
                        four_transposes(lambda n: xn2[:, n % 2, n // 2 * P:(n // 2 + 1) * P], x2T_full)
                    if a and k == AT["p0"]:
                        wait(pe, xnT_ready, a)
                    for j in range(4):
                        if a and k == AT[f"p{j}"]:
                            project(j, a, s, par)
                    for q in range(2):
                        if a and k == AT[f"v{q}"]:
                            project_v(q, a, s, par)
                    if f and k == AT["lg"]:
                        wait_read(pe, TR_USES, "lg", s, 1)
                        wait(pe, x2T_ready, f)
                        for q in range(2):
                            for n in range(2):
                                last = pe.matmul(TR[:, q * E:(q + 1) * E], xn2T[:, n, q * P:(q + 1) * P], wr[:, n, :],
                                                 start=(n == 0), stop=(n == 1))
                        last.then_inc(lg_full, 1)
                    for q in range(2):
                        if d and k == AT[f"n_g{q}"]:
                            norm_T(1, q, d, s)
                        if c and k == AT[f"n_l{q}"]:
                            norm_T(0, q, c, s)
                    if c and k == AT["mT_g"]:
                        maxima_T(1, c, s)
                    if d and k == AT["oT_g"]:
                        out_T(1, d, s)
                    if f and k == AT["cs"]:
                        wait_read(pe, TR_USES, "cs", s, 1)
                        wait(pe, hot_ready, f)
                        pe.matmul(TR[:, 0:E], earlier[:, :], hot[:, 0, :], start=True, stop=True)
                        pe.matmul(TR[:, E:2 * E], earlier[:, :], hot[:, 1, :], start=True, stop=False)
                        pe.matmul(TR[:, E:2 * E], onesb[:, :], hot[:, 0, :], start=False, stop=True)
                        pe.matmul(TR[:, 2 * E:3 * E], onesb[:, :], hot[:, 0, :], start=True, stop=False)
                        pe.matmul(TR[:, 2 * E:3 * E], onesb[:, :], hot[:, 1, :], start=False, stop=True).then_inc(cs_full, 1)
                    if d and k == AT["op"]:
                        wait_read(pe, TR_USES, "op", s, 1)
                        wait(pe, onT_ready[0], d)
                        wait(pe, onT_ready[1], d)
                        for q in range(2):
                            for n in range(4):
                                last = pe.matmul(TR[:, q * D:(q + 1) * D], OnT[:, n // 2, n % 2, q * P:(q + 1) * P], wo[:, n, :],
                                                 start=(n == 0), stop=(n == 3))
                        last.then_inc(o_full, 1)
                    if a and k == AT["mT_l"]:
                        maxima_T(0, a, s)
                    if c and k == AT["oT_l"]:
                        out_T(0, c, s)
                    if a:
                        for u in S1_AT.get(k, ()):
                            row_scores(u, a, par)

            steps(pe, step)

            def transposes(e):
                if eexists(back(e)):
                    pe.wait_ge(eT_ready, eth(back(e)))
                pe.wait_ge(xe_ready, eth(e))
                for c in range(2):
                    for n, (lo, m) in enumerate(CHUNKS):
                        last = pe.transpose(banks[c][:, lo:lo + m], zb[0:m, e[1] % RING, n, c * P:(c + 1) * P], ident[0:m, 0:m])
                last.then_inc(eT_full, 1)

            def gate_up(e):
                pe.wait_ge(gu_in[e[1] % 3], ering(e, 3, 32))
                pe.wait_ge(eT_ready, eth(e))
                for m in range(2):
                    if eexists(back(e)):
                        pe.wait_ge(h_ready, eth(back(e), 2, m))
                    for n in range(2):
                        for c in range(2):
                            last = pe.matmul(banks[2 + 2 * m + n][:, 0:CAP], ew[:, e[1] % 3, n, c, m * P:(m + 1) * P], eT[:, e[1] % 2, c, :],
                                             start=(c == 0), stop=(c == 1))
                    last.then_inc(gu_full, 1)

            def down(e):
                if eexists(back(e)):
                    pe.wait_ge(ze_ready, eth(back(e)))
                pe.wait_ge(down_in[e[1] % 3], ering(e, 3, 16))
                pe.wait_ge(h_ready, eth(e, 2, 1))
                for n, (lo, m) in enumerate(CHUNKS):
                    for c in range(2):
                        last = pe.matmul(banks[6 + n // 2][0:m, n % 2 * D:(n % 2 + 1) * D], hT[:, e[1] % 2, c, lo:lo + m],
                                         ew[:, e[1] % 3, 2, c, :], start=(c == 0), stop=(c == 1))
                last.then_inc(ye_full, 1)

            def expert(e):
                if eexists(e):
                    gate_up(e)
                if eexists(back(e, -1)):
                    transposes(back(e, -1))
                if eexists(back(e)):
                    down(back(e))

            pe.wait_ge(cs_read, NW)
            transposes((None, 0))
            expert_turns(pe, expert, tail=1)


def kernel(**inputs):
    import numpy as np
    import concourse.bacc as bacc
    from concourse.bass_utils import run_bass_kernel_spmd

    arrays = layouts(inputs)
    shape = arrays["x"].shape
    nc = bacc.Bacc("TRN2", target_bir_lowering=False, num_devices=1)
    args = {}
    for name, a in arrays.items():
        args[name] = nc.dram_tensor(name, a.shape, mybir.dt.from_np(a.dtype), kind="ExternalInput").ap()
    args["out"] = nc.dram_tensor("out", shape, mybir.dt.float32, kind="ExternalOutput").ap()
    attention_moe_program(nc, shape[0] * shape[1], **args)
    r = run_bass_kernel_spmd(nc, [arrays], core_ids=[0])
    return r.results[0]["out"]


def layouts(inputs):
    import numpy as np
    a = {n.split("_", 2)[2]: np.ascontiguousarray(v) for n, v in inputs.items()}
    out = {"x": a["x"]}
    for b, name in (("l", "local"), ("g", "global")):
        bias = a[f"b{b}_in"]
        out[f"pT_{b}"] = np.ascontiguousarray(a[f"proj_{name}"].T)
        out[f"winT_{b}"] = np.ascontiguousarray(a[f"W{b}_in"].T)
        out[f"woT_{b}"] = np.ascontiguousarray(a[f"W{b}_out"].T)
        out[f"bqk_{b}"] = np.ascontiguousarray(bias[:512].reshape(2, 2, 8, 16).transpose(3, 2, 0, 1).reshape(128, 4))
        out[f"bv_{b}"] = np.ascontiguousarray(bias[512:].reshape(2, 128).T)
        out[f"bo_{b}"] = a[f"b{b}_out"]
    out["fusion_w"] = a["fusion_w"]
    out["gamma"] = a["ln_gamma"]
    out["beta"] = a["ln_beta"]
    for n in ("w_router", "w_gate", "w_up", "w_down"):
        out[n] = a[n]
    return out
```

```python
import concourse.bass as bass
from concourse import mybir
from contextlib import ExitStack

E_PARTS_Q = (0, 0, 0, 1, 1, 2)
E_PARTS_K = (0, 1, 2, 0, 1, 0)


def attention_moe_program(nc, T, x, pT_l, pT_g, winT_l, winT_g, woT_l, woT_g, bqk_l, bqk_g, bv_l, bv_g,
                          bo_l, bo_g, fusion_w, gamma, beta, w_router, w_gate, w_up, w_down, out):
    f32, bf16, u32 = mybir.dt.float32, mybir.dt.bfloat16, mybir.dt.uint32
    ALU, ACT, AX = mybir.AluOpType, mybir.ActivationFunctionType, mybir.AxisListType

    P = 128
    D = 256
    NH, HD = 16, 16
    WIN = 256
    NW = T // WIN
    E = 32
    CAP = -(-5 * T // (4 * E))
    NSLOT = E * CAP
    EPS = 1e-5
    QSCALE = 0.25
    UNITS = 24
    LU = 8
    GROUPS = 8
    NPART = 6 * HD
    KROWS = NPART + 3
    BROW = KROWS + 1
    CHUNKS = [(r, min(P, CAP - r)) for r in range(0, CAP, P)]
    NCH = len(CHUNKS)
    ROW = D + 4
    MEAN, RSTD, GATE, TOKEN = D, D + 1, D + 2, D + 3
    PIECES = [p_ for p_ in ((0, CAP // P, P), (CAP // P, 1, CAP % P)) if p_[1] * p_[2]]
    ZDMAS = 5
    ZREP = -(-NSLOT // P // ZDMAS)
    RING = 6

    def nth(w, per, k=0):
        i, c = w
        n = c * per + k + 1
        return n if i is None else i * (2 * per) + n

    def back(w, n=1):
        return (w[0], w[1] - n)

    def exists(w):
        return w[0] is not None or 0 <= w[1] < NW

    def num(w):
        return w[1] if w[0] is None else w[0] * 2 + w[1]

    def wait(eng, sem, w, per=1, k=0):
        if exists(w):
            eng.wait_ge(sem, nth(w, per, k))

    x_w = x.rearrange("b s f -> (b s) f").rearrange("(w q p) f -> w p q f", q=2, p=P)
    out_w = out.rearrange("b s f -> (b s) f").rearrange("(w q p) f -> w p q f", q=2, p=P)
    out_t = out.rearrange("b s f -> (b s) f")
    slots_d = nc.dram_tensor("slots_scratch", [NSLOT, ROW], f32).ap()

    with ExitStack() as ctx:
        def sb(name, shape, dt=f32, on=ctx):
            return on.enter_context(nc.sbuf_tensor(name, shape, dt))

        def sem(name):
            return ctx.enter_context(nc.semaphore(name))

        ident = sb("ident", [P, P])
        identb = sb("identb", [P, P], bf16)
        tri = sb("tri", [P, P], bf16)
        earlier = sb("earlier", [P, P], bf16)
        onesb = sb("onesb", [P, P], bf16)
        iota_e = sb("iota_e", [P, E])
        mhalf = sb("mhalf", [P, 4])
        eps2 = sb("eps2", [P, 2])
        minus1 = sb("minus1", [P, 2])
        none = sb("none", [P, 2, NH])
        weff = sb("weff", [P, 2, 2, 3 * D])
        wo = sb("wo", [P, 4, D])
        bqk = sb("bqk", [P, 2, 4])
        bias_row = sb("bias_row", [P, D])
        gamma_row = sb("gamma_row", [P, D])
        beta_row = sb("beta_row", [P, D])
        wr = sb("wr", [P, 2, E])
        behind = sb("behind", [BROW - NPART, 3, 2, P], bf16)
        zeros = sb("zeros", [P, ROW])
        ew = sb("ew", [P, 3, 3, 2, D])
        mv_e = sb("mv_e", [P, 2, NCH, 2])
        ve_e = sb("ve_e", [P, 2, NCH])
        rs_e = sb("rs_e", [P, 2, NCH])
        v_pad = sb("v_pad", [P, 2, 2, 2, NH, 32])
        xw = sb("xw", [P, 2, 2, D])
        xr = sb("xr", [P, 2, 2, D])
        xn = sb("xn", [P, 2, D])
        xnT = sb("xnT", [P, 2, WIN])
        x32 = sb("x32", [P, 2, 512])
        rest = sb("rest", [P, 2, 512])
        parts = sb("parts", [P, 4, 3, 512], bf16)
        mx = sb("mx", [P, 2, 2, NH])
        mneg = sb("mneg", [P, 2, 2, NH])
        mparts = sb("mparts", [P, 2, 2, 3, NH], bf16)
        mT = sb("mT", [48, 2, WIN], bf16)
        OT = sb("OT", [P, 2, 4, WIN])
        rden = sb("rden", [P, 2, NH])
        On = sb("On", [P, 2, 2, D])
        OnT = sb("OnT", [P, 2, 2, WIN])
        fbuf = sb("fbuf", [P, 2, D])
        ybuf = sb("ybuf", [P, 2, D])
        xrow = sb("xrow", [P, 2, ROW])
        x1 = xrow[:, :, 0:D]
        left = sb("left", [P, 2])
        obuf = sb("obuf", [P, 2, D])
        xn2 = sb("xn2", [P, 2, D])
        xn2T = sb("xn2T", [P, 2, WIN])
        bst = sb("bst", [P, 5, 2, 6])
        mv = sb("mv", [P, 5, 2, 2])
        ve = sb("ve", [P, 5, 2])
        nm = sb("nm", [P, 5, 2])
        mr = sb("mr", [P, 5, 2])
        rstd = sb("rstd", [P, 5, 2])
        lg = sb("lg", [P, 2, E])
        top = sb("top", [P, 2, 8])
        top_i = sb("top_i", [P, 2, 8], u32)
        ntop = sb("ntop", [P, 2])
        idx_f = sb("idx_f", [P, 2])
        hot = sb("hot", [P, 2, E], bf16)
        egate = sb("egate", [P, 2, E])
        gsum = sb("gsum", [P, 2])
        base = sb("base", [P, E])
        pos = sb("pos", [P, 2, E])
        posh = sb("posh", [P, 2, E])
        pos1 = sb("pos1", [P, 2])
        okf = sb("okf", [P, 2])
        slotf = sb("slotf", [P, 2])
        far = sb("far", [P, 2])
        gate1 = sb("gate1", [P, 2])
        slot_u = sb("slot_u", [P, 2], u32)
        with ExitStack() as prep:
            pT = sb("pT", [P, 2, 2, D], on=prep)
            winT = sb("winT", [P, 2, 2, 3 * D], on=prep)
            bv = sb("bv", [P, 4], on=prep)
            bvb = sb("bvb", [P, 4, P], on=prep)
            bo = sb("bo", [P, 2, D], on=prep)
            fus = sb("fus", [P, 2], on=prep)
            fus_e = sb("fus_e", [P, 2], on=prep)
            fus_m = sb("fus_m", [P, 2], on=prep)
        with ExitStack() as attn:
            pt = sb("pt", [P, 8, 512], on=attn)
            stack = sb("stack", [P, 2, 2, 2, 8, 2, WIN], bf16, on=attn)
        with ExitStack() as experts:
            erows = sb("erows", [P, RING, NCH, ROW], on=experts)
            zb = sb("zb", [P, RING, NCH, D], on=experts)
            idx_e = sb("idx_e", [P, RING, NCH], u32, on=experts)
            eT = sb("eT", [P, 2, 2, CAP], on=experts)
            sg = sb("sg", [P, 2, CAP], on=experts)
            hT = sb("hT", [P, 2, 2, CAP], on=experts)
            bst_e = sb("bst_e", [P, NCH, 6], on=experts)

        banks = [ctx.enter_context(nc.psum_tensor(f"bank{n}", [P, 512], f32)) for n in range(8)]
        S2, PV, PJ, TR = banks[2:4], banks[4], banks[5:7], banks[7]
        S1 = PJ + banks[0:2]

        w_in = [sem("w_in_l"), sem("w_in_g")]
        wo_in = sem("wo_in")
        behind_in = sem("behind_in")
        w_fold = sem("w_fold")
        w_fold_out = sem("w_fold_out")
        fus_sem = sem("fus_sem")
        fus_exp = sem("fus_exp")
        wo_ready = sem("wo_ready")
        bias_ps = sem("bias_ps")
        const_pool = sem("const_pool")
        const_dve = sem("const_dve")
        zeroed = sem("zeroed")
        x_in = [sem("x_in0"), sem("x_in1")]
        xr_in = [sem("xr_in0"), sem("xr_in1")]
        ln_var = [sem(f"ln_var{n}") for n in range(5)]
        ln_rstd = [sem(f"ln_rstd{n}") for n in range(5)]
        xn_ready = sem("xn_ready")
        xnT_full = sem("xnT_full")
        xnT_ready = sem("xnT_ready")
        pj_full = sem("pj_full")
        v_full = sem("v_full")
        x32_ready = sem("x32_ready")
        rest_ready = sem("rest_ready")
        mid_ready = sem("mid_ready")
        lo_ready = sem("lo_ready")
        spread = [sem(f"spread{n}") for n in range(4)]
        v_ready = sem("v_ready")
        s1_full = sem("s1_full")
        s1_read = sem("s1_read")
        mparts_ready = [sem("mparts_l"), sem("mparts_g")]
        mT_full = [sem("mT_full_l"), sem("mT_full_g")]
        mT_ready = [sem("mT_ready_l"), sem("mT_ready_g")]
        m_in = [sem("m_in_l"), sem("m_in_g")]
        s2_full = sem("s2_full")
        p_ready = sem("p_ready")
        pv_full = sem("pv_full")
        ot_ready = sem("ot_ready")
        nrm_full = [sem("nrm_full_l"), sem("nrm_full_g")]
        on_ready = [sem("on_ready_l"), sem("on_ready_g")]
        onT_full = [sem("onT_full_l"), sem("onT_full_g")]
        onT_ready = [sem("onT_ready_l"), sem("onT_ready_g")]
        o_full = sem("o_full")
        f_ready = sem("f_ready")
        n1_ready = sem("n1_ready")
        y_ready = sem("y_ready")
        z_ready = sem("z_ready")
        x1_ready = sem("x1_ready")
        o_norm = sem("o_norm")
        o_ready = sem("o_ready")
        o_out = sem("o_out")
        xn2_ready = sem("xn2_ready")
        x2T_full = sem("x2T_full")
        x2T_ready = sem("x2T_ready")
        lg_full = sem("lg_full")
        lg_ready = sem("lg_ready")
        hot_ready = sem("hot_ready")
        gsum_ready = sem("gsum_ready")
        cs_full = sem("cs_full")
        cs_read = sem("cs_read")
        slot_ready = sem("slot_ready")
        scat = sem("scat")

        gu_in = [sem(f"gu_in{n}") for n in range(3)]
        down_in = [sem(f"down_in{n}") for n in range(3)]
        er_in = [sem(f"er_in{n}") for n in range(RING)]
        xe_ready = sem("xe_ready")
        eT_full = sem("eT_full")
        eT_ready = sem("eT_ready")
        gu_full = sem("gu_full")
        sg_ready = sem("sg_ready")
        h_ready = sem("h_ready")
        ye_full = sem("ye_full")
        ze_ready = sem("ze_ready")
        ve_ready = sem("ve_ready")
        rs_ready = sem("rs_ready")
        ne_ready = sem("ne_ready")
        oe_ready = sem("oe_ready")
        oe_out = [sem(f"oe_out{n}") for n in range(RING)]

        TR_USES = [("x2T", 3, x2T_ready, 1, 0), ("lg", 3, lg_ready, 1, 0), ("n_g0", 2, on_ready[1], 2, 0),
                   ("n_g1", 2, on_ready[1], 2, 1), ("mT_g", 1, mT_ready[1], 1, 0), ("oT_g", 2, onT_ready[1], 1, 0),
                   ("cs", 3, cs_read, 1, 0), ("op", 2, f_ready, 1, 0), ("mT_l", 0, mT_ready[0], 1, 0),
                   ("n_l0", 1, on_ready[0], 2, 0), ("n_l1", 1, on_ready[0], 2, 1), ("oT_l", 1, onT_ready[0], 1, 0)]
        PJ_USES = [("xnT", 0, xnT_ready, 1, 0), ("p0", 0, x32_ready, 4, 0), ("p1", 0, x32_ready, 4, 1),
                   ("p2", 0, x32_ready, 4, 2), ("p3", 0, x32_ready, 4, 3), ("v0", 0, v_ready, 2, 0),
                   ("v1", 0, v_ready, 2, 1)]
        AT = {"xnT": 0, "x2T": 0, "split_g": 0, "p0": 1, "lg": 1, "p1": 2, "top": 2, "o_norm": 2, "p2": 3, "n_g0": 3,
              "p3": 4, "n_g1": 4, "norm0": 4, "v0": 5, "mT_g": 5, "gate": 5, "v1": 6, "oT_g": 6, "cs": 7, "op": 8,
              "f1": 10, "stats_y": 12, "mT_l": 14, "n_l0": 16, "z": 16, "n_l1": 18, "stats_x1": 18, "oT_l": 20,
              "xn2": 20, "stats_xn2": 22}
        GROUP_AT = {3: 0, 5: 1, 7: 2, 9: 3, 13: 4, 17: 5, 21: 6}
        LAST_GROUP_AT = 1
        S1_AT = {**{k: (2 * k - 14, 2 * k - 13) for k in range(7, 14)}, **{k: (k,) for k in range(14, UNITS)}}

        def wait_alone(eng, sem, value):
            if not isinstance(value, int):
                value = eng.to_reg(value)
            eng.wait_ge(const_pool, 1)
            eng.wait_ge(sem, value)

        def read_before(uses, name, s, ago):
            at = [u[0] for u in uses].index(name)
            step, left = s, ago
            while left:
                at -= 1
                if at < 0:
                    at, step = len(uses) - 1, back(step)
                    if step[0] is None and step[1] < 0:
                        return None
                w = back(step, uses[at][1])
                left -= exists(w)
            return uses[at][2], nth(w, uses[at][3], uses[at][4])

        def wait_read(eng, uses, name, s, ago):
            before = read_before(uses, name, s, ago)
            if before:
                eng.wait_ge(*before)

        def pj_bank(name):
            return PJ[[u[0] for u in PJ_USES].index(name) % 2]

        def steps(eng, one):
            for s in range(4):
                one((None, s), s % 2)
            with eng.Fori(0, (NW - 6) // 2) as i:
                one((i, 4), 0)
                one((i, 5), 1)
            for s in range(NW - 2, NW + 3):
                one((None, s), s % 2)

        def expert_turns(eng, one, tail=0):
            turns = (E - RING) // RING
            for e in range(RING):
                one((None, e))
            with eng.Fori(0, turns) as i:
                for n in range(RING):
                    one((i, RING + n))
            for e in range(RING * (turns + 1), E + tail):
                one((None, e))

        def eexists(e):
            return e[0] is not None or 0 <= e[1] < E

        def eth(e, per=1, k=0):
            i, n = e
            n = n * per + k + 1
            return n if i is None else i * (RING * per) + n

        def ering(e, size, per):
            i, n = e
            n = per * (n // size + 1)
            return n if i is None else i * (RING // size * per) + n

        def enum(e):
            return e[1] if e[0] is None else e[0] * RING + e[1]

        def alternate(w, per):
            i, n = w
            n = per * (n // 2 + 1)
            return n if i is None else i * per + n

        def stages(s):
            return [w if exists(w) else None for w in (s, back(s, 1), back(s, 2), back(s, 3))]

        def q_stack(par, b, h, lo, n, rows=KROWS):
            return stack[0:rows, par, b, 0, h % 8, h // 8, lo:lo + n]

        def k_stack(par, b, h, lo, n, rows=KROWS):
            return stack[0:rows, par, b, 1, h % 8, h // 8, lo:lo + n]

        ACT_NORMS = (1, 2, 4)

        block = ctx.enter_context(nc.Block())

        @block.sync
        def _(sp):
            for b, (p_, w_) in enumerate(((pT_l, winT_l), (pT_g, winT_g))):
                sp.dma_start(pT[:, b, :, :], p_.rearrange("(c p) n -> p c n", p=P)).then_inc(w_in[b], 16)
                sp.dma_start(winT[:, b, :, :], w_.rearrange("(c p) n -> p c n", p=P)).then_inc(w_in[b], 16)
            sp.dma_start(xw[:, 1, :, :], x_w[1]).then_inc(x_in[1], 16)
            sp.dma_start(gamma_row[:, :], gamma.partition_broadcast(P)).then_inc(wo_in, 16)
            sp.dma_start(beta_row[:, :], beta.partition_broadcast(P)).then_inc(wo_in, 16)
            sp.dma_start(wr[:, :, :], w_router.rearrange("(c p) n -> p c n", p=P)).then_inc(wo_in, 16)
            sp.wait_ge(w_fold, 8)
            sp.wait_ge(bias_ps, 1)
            sp.wait_ge(const_dve, 1)
            sp.wait_ge(const_pool, 1)
            for p_ in range(2):
                for kind, (b, qk, lo, hi) in enumerate(((0, 1, NPART, KROWS), (1, 1, NPART, BROW), (1, 0, KROWS, BROW))):
                    sp.dma_start(stack[lo:hi, p_, b, qk, :, :, :].rearrange("r h t n -> r (h t) n"),
                                 behind[lo - NPART:hi - NPART, kind, :, :].rearrange("r a n -> r (a n)").unsqueeze(1).to_broadcast([hi - lo, NH, WIN])
                                 ).then_inc(behind_in, 16)

            def zero_slots(n):
                dst = slots_d.rearrange("(p g) f -> p g f", p=P)[:, n * ZREP:min((n + 1) * ZREP, NSLOT // P), :]
                sp.dma_start(dst, zeros[:, :].unsqueeze(1).to_broadcast(list(dst.shape))).then_inc(zeroed, 16)

            def expert_weights(e):
                r, before = e[1] % 3, (e[0], e[1] - 3)
                if eexists(before):
                    wait_alone(sp, gu_full, eth(before, 2, 1))
                for n in range(3):
                    if n == 2 and eexists(before):
                        wait_alone(sp, ye_full, eth(before))
                    sp.dma_start(ew[:, r, n, :, :], w_e[n][bass.ds(enum(e), 1)].rearrange("e p c f -> (e p) c f")
                                 ).then_inc((gu_in, gu_in, down_in)[n][r], 16)

            w_e = [w.rearrange("e (c p) f -> e p c f", p=P) for w in (w_gate, w_up, w_down)]

            def spread_parts(j, a, par):
                b, qk = j // 2, j % 2
                for part, ready in enumerate((x32_ready, mid_ready, lo_ready)):
                    wait_alone(sp, ready, nth(a, 4, j))
                    for g in range(6):
                        if (E_PARTS_Q, E_PARTS_K)[qk][g] == part:
                            sp.dma_start(stack[HD * g:HD * g + HD, par, b, qk, :, :, :].rearrange("d h t n -> d h (t n)"),
                                         parts[:, j, part, :]).then_inc(spread[j], 16)

            def maxima_in(b, w, par):
                wait_alone(sp, mT_ready[b], nth(w, 1))
                sp.dma_start(stack[NPART:KROWS, par, b, 0, :, :, :].rearrange("r h t n -> r (h t) n"), mT[:, b, :]
                             ).then_inc(m_in[b], 16)

            def step(s, par):
                a, c, d, f = stages(s)
                ahead = back(s, -2)
                if a and (ahead[0] is not None or ahead[1] < NW):
                    wait_alone(sp, xn_ready, nth(a, 1))
                    sp.dma_start(xw[:, par, :, :], x_w[bass.ds(num(ahead), 1)].rearrange("w p q f -> (w p) q f")
                                 ).then_inc(x_in[par], 16)
                if a:
                    if exists(back(a, 2)):
                        wait_alone(sp, s2_full, nth(back(a, 2), UNITS, UNITS - 1))
                    spread_parts(0, a, par)
                    spread_parts(1, a, par)
                if c:
                    maxima_in(1, c, 1 - par)
                if a:
                    spread_parts(2, a, par)
                    spread_parts(3, a, par)
                if d:
                    if exists(back(d, 2)):
                        wait_alone(sp, x1_ready, nth(back(d, 2), 1))
                    sp.dma_start(xr[:, par, :, :], x_w[bass.ds(num(d), 1)].rearrange("w p q f -> (w p) q f")
                                 ).then_inc(xr_in[par], 16)
                if f:
                    wait_alone(sp, o_ready, nth(f, 1))
                    sp.dma_start(out_w[bass.ds(num(f), 1)].rearrange("w p q f -> (w p) q f"), obuf[:, :, :]).then_inc(o_out, 16)
                if a:
                    maxima_in(0, a, par)
                if s[0] is None and s[1] < 3:
                    for n in range(s[1], ZDMAS, 3):
                        zero_slots(n)
                if s[0] is None and s[1] == NW - 2:
                    for e in range(3):
                        expert_weights((None, e))

            steps(sp, step)

            sp.wait_ge(pv_full, GROUPS * NW)
            sp.wait_ge(scat, 32 * NW)
            rows_e = slots_d.rearrange("(e r) f -> e r f", e=E)

            def expert(e):
                r, before = e[1] % RING, (e[0], e[1] - RING)
                if eexists(before):
                    wait_alone(sp, oe_ready, eth(before))
                for n, (lo, m) in enumerate(CHUNKS):
                    sp.dma_start(erows[0:m, r, n, :], rows_e[bass.ds(enum(e), 1), lo:lo + m, :].rearrange("e r f -> (e r) f")
                                 ).then_inc(er_in[r], 16)
                if e[0] is not None or e[1] >= 3:
                    expert_weights(e)

            expert_turns(sp, expert)
            sp.wait_ge(o_out, 16 * NW)
            for r in range(RING):
                sp.wait_ge(oe_out[r], 16 * NCH * len(range(r, E, RING)))

        @block.gpsimd
        def _(pool):
            pool.memset(ident[:, :], 0.0)
            pool.memset(identb[:, :], 0.0)
            pool.memset(tri[:, :], 1.0)
            pool.memset(earlier[:, :], 1.0)
            pool.memset(onesb[:, :], 1.0)
            pool.memset(mhalf[:, :], -0.5)
            pool.memset(eps2[:, :], EPS)
            pool.memset(minus1[:, :], -1.0)
            pool.memset(none[:, :, :], 0.0)
            pool.iota(left[:, :], pattern=[[-P, 2]], base=T, channel_multiplier=-1, allow_small_or_imprecise_dtypes=True)
            pool.iota(iota_e[:, :], pattern=[[1, E]], base=0, channel_multiplier=0, allow_small_or_imprecise_dtypes=True)
            pool.drain()
            for m in (ident, identb):
                pool.affine_select(out=m[:, :], in_=m[:, :], compare_op=ALU.not_equal, fill=1.0,
                                   base=0, pattern=[[-1, P]], channel_multiplier=1)
            pool.affine_select(out=tri[:, :], in_=tri[:, :], compare_op=ALU.is_gt, fill=0.0,
                               base=0, pattern=[[-1, P]], channel_multiplier=1)
            pool.affine_select(out=earlier[:, :], in_=earlier[:, :], compare_op=ALU.is_gt, fill=0.0,
                               base=0, pattern=[[1, P]], channel_multiplier=-1)
            pool.memset(behind[:, :, :, :], 1.0)
            pool.drain()
            for kind, tile in ((1, 0), (2, 1)):
                pool.affine_select(out=behind[:, kind, tile, :], in_=behind[:, kind, tile, :], compare_op=ALU.not_equal, fill=0.0,
                                   base=-(BROW - 1 - NPART), pattern=[[0, P]], channel_multiplier=1)
            pool.drain().then_inc(const_pool, 1)

            def inv_std(n, w):
                wait(pool, ln_var[n], w)
                pool.tensor_tensor(ve[:, n, :], mv[:, n, :, 1], eps2[:, :], ALU.add)
                if n in ACT_NORMS:
                    pool.tensor_tensor(nm[:, n, :], mv[:, n, :, 0], minus1[:, :], ALU.mult)
                pool.drain()
                last = pool.tensor_tensor(rstd[:, n, :], ve[:, n, :], mhalf[:, 0:2], ALU.pow)
                if n in ACT_NORMS:
                    pool.drain()
                    last = pool.tensor_tensor(mr[:, n, :], nm[:, n, :], rstd[:, n, :], ALU.mult)
                last.then_inc(ln_rstd[n], 1)

            def split_local_maxima(a):
                wait(pool, s1_read, a, UNITS, LU - 1)
                wait(pool, mT_full[0], back(a))
                pool.tensor_tensor(mneg[:, 0, :, :], none[:, :, :], mx[:, 0, :, :], ALU.subtract)
                pool.tensor_tensor(mparts[:, 0, :, 0, :], none[:, :, :], mx[:, 0, :, :], ALU.subtract)
                pool.drain()
                pool.tensor_tensor(mneg[:, 0, :, :], mneg[:, 0, :, :], mparts[:, 0, :, 0, :], ALU.subtract)
                pool.drain()
                pool.tensor_tensor(mparts[:, 0, :, 1, :], mneg[:, 0, :, :], none[:, :, :], ALU.add)
                pool.drain()
                pool.tensor_tensor(mparts[:, 0, :, 2, :], mneg[:, 0, :, :], mparts[:, 0, :, 1, :], ALU.subtract
                                   ).then_inc(mparts_ready[0], 1)

            def remainder(j, a):
                wait(pool, x32_ready, a, 4, j)
                if j < 2:
                    wait(pool, mid_ready, back(a), 4, j + 2)
                else:
                    wait(pool, mid_ready, a, 4, j - 2)
                pool.tensor_tensor(rest[:, j % 2, :], x32[:, j % 2, :], parts[:, j, 0, :], ALU.subtract
                                   ).then_inc(rest_ready, 1)

            def low_part(j, a):
                wait(pool, mid_ready, a, 4, j)
                pool.tensor_tensor(parts[:, j, 2, :], rest[:, j % 2, :], parts[:, j, 1, :], ALU.subtract
                                   ).then_inc(lo_ready, 1)

            def step(s, par):
                a, c, d, f = stages(s)
                nxt = back(s, -1)
                if a:
                    for j in range(4):
                        remainder(j, a)
                        if j == 3 and (nxt[0] is not None or nxt[1] < NW):
                            inv_std(0, nxt)
                        low_part(j, a)
                if f:
                    wait(pool, o_norm, f)
                    pool.tensor_tensor(obuf[:, :, :], obuf[:, :, :], x1[:, :, :], ALU.add).then_inc(o_ready, 1)
                    pool.wait_ge(zeroed, 16 * ZDMAS)
                    wait_alone(pool, slot_ready, nth(f, 1))
                    for q in range(2):
                        pool.indirect_dma_start(
                            out=slots_d, out_offset=bass.IndirectOffsetOnAxis(ap=slot_u[:, q:q + 1], axis=0),
                            in_=xrow[:, q, :], in_offset=None, bounds_check=NSLOT - 1, oob_is_err=False).then_inc(scat, 16)
                if d:
                    inv_std(1, d)
                    wait(pool, n1_ready, d)
                    pool.tensor_tensor(ybuf[:, :, :], fbuf[:, :, :], gamma_row[:, :].unsqueeze(1).to_broadcast([P, 2, D]), ALU.mult)
                    pool.drain()
                    pool.tensor_tensor(ybuf[:, :, :], ybuf[:, :, :], beta_row[:, :].unsqueeze(1).to_broadcast([P, 2, D]), ALU.add
                                       ).then_inc(y_ready, 1)
                if a:
                    split_local_maxima(a)
                if d:
                    inv_std(2, d)
                    wait(pool, z_ready, d)
                    if exists(back(d)):
                        pool.wait_ge(scat, nth(back(d), 32, 31))
                    wait(pool, xn2_ready, back(d))
                    pool.wait_ge(xr_in[par], xr_count(d))
                    pool.tensor_tensor(x1[:, :, :], ybuf[:, :, :], xr[:, par, :, :], ALU.add).then_inc(x1_ready, 1)
                    inv_std(3, d)
                    inv_std(4, d)

            def xr_count(d):
                i, n = d
                n = 16 * (n // 2 + 1)
                return n if i is None else i * 16 + n

            inv_std(0, (None, 0))
            steps(pool, step)

            pool.wait_ge(o_out, 16 * NW)

            def expert(e):
                last, old = back(e), back(e, 2)
                if eexists(old):
                    r = old[1] % RING
                    pool.wait_ge(ne_ready, eth(old))
                    for lo, n, m in PIECES:
                        done = pool.tensor_tensor(zb[0:m, r, lo:lo + n, :], zb[0:m, r, lo:lo + n, :],
                                                  erows[0:m, r, lo:lo + n, 0:D], ALU.add)
                    done.then_inc(oe_ready, 1)
                    wait_alone(pool, oe_ready, eth(old))
                    for n, (lo, m) in enumerate(CHUNKS):
                        pool.indirect_dma_start(
                            out=out_t, out_offset=bass.IndirectOffsetOnAxis(ap=idx_e[0:m, r, n:n + 1], axis=0),
                            in_=zb[0:m, r, n, :], in_offset=None, bounds_check=T - 1, oob_is_err=False).then_inc(oe_out[r], 16)
                if eexists(last):
                    pool.wait_ge(ve_ready, eth(last))
                    pool.tensor_tensor(rs_e[:, last[1] % 2, :], ve_e[:, last[1] % 2, :], mhalf[:, 0:NCH], ALU.pow
                                       ).then_inc(rs_ready, 1)

            expert_turns(pool, expert, tail=2)

        @block.scalar
        def _(act):
            act.dma_start(xw[:, 0, :, :], x_w[0]).then_inc(x_in[0], 16)
            act.dma_start(fus[:, :], fusion_w.partition_broadcast(P)).then_inc(wo_in, 16)
            for b, (o_, k_, v_, c_) in enumerate(((woT_l, bqk_l, bv_l, bo_l), (woT_g, bqk_g, bv_g, bo_g))):
                act.dma_start(bv[:, 2 * b:2 * b + 2], v_).then_inc(wo_in, 16)
                act.dma_start(bqk[:, b, :], k_).then_inc(wo_in, 16)
                act.dma_start(wo[:, 2 * b:2 * b + 2, :], o_.rearrange("(c p) n -> p c n", p=P)).then_inc(wo_in, 16)
                act.dma_start(bo[:, b, :], c_.partition_broadcast(P)).then_inc(wo_in, 16)
            act.wait_ge(fus_sem, 1)
            act.activation(fus_e[:, :], fus[:, :], ACT.Exp, bias=fus_m[:, 0:1]).then_inc(fus_exp, 1)
            n = 0
            for b in range(2):
                for c in range(2):
                    act.wait_ge(w_fold, n + 1)
                    act.activation(weff[:, b, c, 0:512].rearrange("p (x d h) -> p x d h", d=HD, h=8),
                                   banks[n][:, :].rearrange("p (x h d) -> p x d h", d=HD, h=8), ACT.Copy)
                    act.wait_ge(w_fold, n + 2)
                    act.activation(weff[:, b, c, 512:768], banks[n + 1][:, 0:256], ACT.Copy).then_inc(w_fold_out, 1)
                    n += 2

            def exps(u, c):
                wait(act, s2_full, c, UNITS, u)
                if u < 8:
                    wait(act, pv_full, back(c), GROUPS, 6 + u // 4)
                elif u < 16:
                    wait(act, pv_full, c, GROUPS, (u - 8) // 2)
                else:
                    wait(act, pv_full, c, GROUPS, 4 + (u - 16) // 4)
                act.activation(pt[:, u % 8, :], S2[u % 2][:, :], ACT.Exp).then_inc(p_ready, 1)

            def values_out(g, c):
                wait(act, pv_full, c, GROUPS, g)
                b = g // 4
                wait(act, nrm_full[b], back(c), 2, 1)
                act.activation(OT[:, b, g % 4, :], PV[:, 0:WIN], ACT.Copy).then_inc(ot_ready, 1)

            def projected(j, a, par):
                wait(act, pj_full, a, 4, j)
                wait(act, rest_ready, a if j >= 2 else back(a), 4, (j - 2) % 4)
                if exists(back(a)):
                    act.wait_ge(spread[j], nth(back(a), 96, 95))
                b, qk = j // 2, j % 2
                bank = pj_bank(f"p{j}")
                for dst in (parts[:, j, 0, :], x32[:, j % 2, :]):
                    for t in range(2):
                        last = act.activation(dst[:, t * WIN:(t + 1) * WIN], bank[:, t * WIN:(t + 1) * WIN], ACT.Identity,
                                              bias=bqk[:, b, 2 * qk + t:2 * qk + t + 1], scale=QSCALE if qk == 0 else 1.0)
                last.then_inc(x32_ready, 1)

            def v_out(q, a, par):
                wait(act, v_full, a, 2, q)
                wait(act, pv_full, back(a, 2), GROUPS, GROUPS - 1)
                act.activation(v_pad[:, par, q, :, :, 0:HD],
                               pj_bank(f"v{q}")[:, :].rearrange("p (b h d) -> p b h d", b=2, d=HD), ACT.Copy
                               ).then_inc(v_ready, 1)

            def norm(n, dst, src, sem_, w):
                wait(act, ln_rstd[n], w)
                for q in range(2):
                    last = act.activation(dst[:, q, :], src[:, q, :], ACT.Identity, bias=mr[:, n, q:q + 1], scale=rstd[:, n, q:q + 1])
                last.then_inc(sem_, 1)

            def maxima_out(b, a):
                wait(act, mT_full[b], a)
                if exists(back(a)):
                    act.wait_ge(m_in[b], nth(back(a), 16, 15))
                act.activation(mT[:, b, :], TR[0:48, 0:WIN // 2].bitcast(bf16), ACT.Copy).then_inc(mT_ready[b], 1)

            def onT_out(b, w):
                wait(act, onT_full[b], w)
                wait(act, o_full, back(w))
                act.activation(OnT[:, b, :, :].rearrange("p t n -> p (t n)"), TR[:, :], ACT.Copy).then_inc(onT_ready[b], 1)

            def step(s, par):
                a, c, d, f = stages(s)
                for k in range(UNITS):
                    if c:
                        exps(k, c)
                        if k in GROUP_AT:
                            values_out(GROUP_AT[k], c)
                    if d and k == LAST_GROUP_AT:
                        values_out(GROUPS - 1, d)
                    if a and k == AT["xnT"]:
                        wait(act, xnT_full, a)
                        wait(act, v_full, back(a), 2, 1)
                        act.activation(xnT[:, :, :].rearrange("p c n -> p (c n)"), pj_bank("xnT")[:, :], ACT.Copy
                                       ).then_inc(xnT_ready, 1)
                    if f and k == AT["x2T"]:
                        wait(act, x2T_full, f)
                        act.activation(xn2T[:, :, :].rearrange("p c n -> p (c n)"), TR[:, :], ACT.Copy).then_inc(x2T_ready, 1)
                    for j in range(4):
                        if a and k == AT[f"p{j}"]:
                            projected(j, a, par)
                    if f and k == AT["o_norm"]:
                        if exists(back(f)):
                            act.wait_ge(o_out, nth(back(f), 16, 15))
                        norm(4, obuf, xn2, o_norm, f)
                    if d and k == AT["f1"]:
                        norm(1, fbuf, fbuf, n1_ready, d)
                    if d and k == AT["z"]:
                        norm(2, ybuf, ybuf, z_ready, d)
                    if c and k == AT["mT_g"]:
                        maxima_out(1, c)
                    for q in range(2):
                        if a and k == AT[f"v{q}"]:
                            v_out(q, a, par)
                    if d and k == AT["oT_g"]:
                        onT_out(1, d)
                    if f and k == AT["gate"]:
                        wait(act, lg_ready, f)
                        for q in range(2):
                            last = act.activation(egate[:, q, :], lg[:, q, :], ACT.Exp, bias=ntop[:, q:q + 1],
                                                  accum_out=gsum[:, q:q + 1])
                        last.then_inc(gsum_ready, 1)
                    if a and k == AT["mT_l"]:
                        maxima_out(0, a)
                    if c and k == AT["oT_l"]:
                        onT_out(0, c)

            steps(act, step)

            def transposed(e):
                act.wait_ge(eT_full, eth(e))
                for c in range(2):
                    last = act.activation(eT[:, e[1] % 2, c, :], banks[c][:, 0:CAP], ACT.Copy)
                last.then_inc(eT_ready, 1)

            def expert(e):
                for m in range(2):
                    act.wait_ge(gu_full, eth(e, 2, m))
                    if eexists(back(e)):
                        act.wait_ge(h_ready, eth(back(e), 2, m))
                    act.activation(sg[:, m, :], banks[2 + 2 * m][:, 0:CAP], ACT.Silu).then_inc(sg_ready, 1)
                if eexists(back(e, -1)):
                    transposed(back(e, -1))

            transposed((None, 0))
            expert_turns(act, expert)

        @block.vector
        def _(dve):
            dve.memset(zeros[:, :], 0.0)
            dve.memset(base[:, :], 0.0)
            dve.memset(mv_e[:, :, :, :], 0.0)
            dve.memset(v_pad[:, :, :, :, :, :], 0.0)
            dve.drain()
            for p_ in range(2):
                for q in range(2):
                    for b in range(2):
                        dve.memset(v_pad[:, p_, q, b, :, HD:HD + 1], 1.0)
            dve.drain().then_inc(const_dve, 1)
            def stats(n, src, w):
                for q in range(2):
                    dve.bn_stats(bst[:, n, q, :], src[:, q, :])
                dve.drain()
                for q in range(2):
                    last = dve.bn_aggr(mv[:, n, q, :], bst[:, n, q, :])
                last.then_inc(ln_var[n], 1)

            def norm(n, dst, src, sem, w):
                wait(dve, ln_rstd[n], w)
                for q in range(2):
                    last = dve.tensor_scalar(dst[:, q, :], src[:, q, :], mv[:, n, q, 0:1], rstd[:, n, q:q + 1],
                                             ALU.subtract, ALU.mult)
                last.then_inc(sem, 1)

            def first_stats(w, par):
                dve.wait_ge(x_in[par], alternate(w, 16))
                stats(0, xw[:, par, :, :], w)

            def first_norm(w, par):
                wait(dve, xnT_full, back(w))
                norm(0, xn, xw[:, par, :, :], xn_ready, w)

            first_stats((None, 0), 0)
            first_norm((None, 0), 0)
            dve.wait_ge(wo_in, 16 * 12)
            dve.tensor_copy(bvb[:, :, :], bv[:, :].unsqueeze(2).to_broadcast([P, 4, P]))
            dve.reduce_max(fus_m[:, 1:2], fus[:, :], AX.X)
            dve.tensor_scalar(bqk[:, :, 0:2], bqk[:, :, 0:2], QSCALE, None, ALU.mult)
            dve.drain()
            dve.tensor_scalar(fus_m[:, 0:1], fus_m[:, 1:2], -1.0, None, ALU.mult).then_inc(fus_sem, 1)
            dve.wait_ge(fus_exp, 1)
            dve.reduce_sum(fus_m[:, 1:2], fus_e[:, :], AX.X)
            dve.drain()
            dve.reciprocal(fus_m[:, 1:2], fus_m[:, 1:2])
            dve.drain()
            dve.tensor_scalar(fus_e[:, :], fus_e[:, :], fus_m[:, 1:2], None, ALU.mult)
            dve.drain()
            for b in range(2):
                dve.tensor_scalar(wo[:, 2 * b:2 * b + 2, :], wo[:, 2 * b:2 * b + 2, :], fus_e[:, b:b + 1], None, ALU.mult)
                dve.tensor_scalar(bo[:, b, :], bo[:, b, :], fus_e[:, b:b + 1], None, ALU.mult)
            dve.drain()
            dve.tensor_tensor(bias_row[:, :], bo[:, 0, :], bo[:, 1, :], ALU.add).then_inc(wo_ready, 1)
            dve.wait_ge(bias_ps, 1)
            dve.drain()
            dve.tensor_tensor(bias_row[:, :], TR[:, 0:D], bias_row[:, :], ALU.add)
            dve.drain().then_inc(const_dve, 1)

            def mid_part(j, a):
                wait(dve, rest_ready, a, 4, j)
                dve.tensor_copy(parts[:, j, 1, :], rest[:, j % 2, :]).then_inc(mid_ready, 1)

            def maximum(u, a):
                if u == 0:
                    wait(dve, mparts_ready[0], back(a))
                wait(dve, s1_full, a, UNITS, u)
                if u < LU:
                    dst = mx[:, 0, :, :].rearrange("p q (h t) -> p t h q", t=2)[:, u // 4, (2 * u) % 8:(2 * u) % 8 + 2, :]
                    src = S1[u % 4][:, :].rearrange("p (h q n) -> p h q n", h=2, q=2)
                else:
                    h = u - LU
                    dst = mx[:, 1, :, 2 * (h % 8) + h // 8]
                    src = S1[u % 4][:, :].rearrange("p (q n) -> p q n", q=2)
                dve.reduce_max(dst, src, AX.X).then_inc(s1_read, 1)

            def split_global_maxima(a):
                dve.drain()
                wait(dve, mT_full[1], back(a))
                dve.tensor_scalar(mparts[:, 1, :, 0, :], mx[:, 1, :, :], -1.0, None, ALU.mult)
                dve.drain()
                dve.scalar_tensor_tensor(mneg[:, 1, :, :], mx[:, 1, :, :], -1.0, mparts[:, 1, :, 0, :], ALU.mult, ALU.subtract)
                dve.drain()
                dve.tensor_copy(mparts[:, 1, :, 1, :], mneg[:, 1, :, :])
                dve.drain()
                dve.tensor_tensor(mparts[:, 1, :, 2, :], mneg[:, 1, :, :], mparts[:, 1, :, 1, :], ALU.subtract
                                  ).then_inc(mparts_ready[1], 1)

            def normalise(b, q, w):
                wait(dve, nrm_full[b], w, 2, q)
                src = TR[:, :].rearrange("p (h m) -> p h m", m=32)
                dve.reciprocal(rden[:, b, :], src[:, :, HD])
                dve.drain()
                wait(dve, onT_full[b], back(w))
                dve.tensor_tensor(On[:, b, q, :].rearrange("p (h d) -> p h d", d=HD), src[:, :, 0:HD],
                                  rden[:, b, :].unsqueeze(2).to_broadcast([P, NH, HD]), ALU.mult).then_inc(on_ready[b], 1)

            def route_top(d):
                wait(dve, lg_full, d)
                wait(dve, gsum_ready, back(d))
                dve.tensor_copy(lg[:, :, :], TR[:, 0:2 * E].rearrange("p (q e) -> p q e", q=2))
                dve.drain()
                for q in range(2):
                    dve.max(top[:, q, :], lg[:, q, :])
                dve.drain()
                dve.tensor_scalar(ntop[:, :], top[:, :, 0], -1.0, None, ALU.mult).then_inc(lg_ready, 1)
                for q in range(2):
                    dve.max_index(top_i[:, q, :], top[:, q, :], lg[:, q, :])
                dve.drain()
                dve.tensor_copy(idx_f[:, :], top_i[:, :, 0])
                dve.drain()
                wait(dve, cs_full, back(d))
                for q in range(2):
                    last = dve.tensor_scalar(hot[:, q, :], iota_e[:, :], idx_f[:, q:q + 1], None, ALU.is_equal)
                last.then_inc(hot_ready, 1)

            def route_slot(d):
                wait(dve, cs_full, d)
                dve.tensor_tensor(pos[:, :, :], TR[:, 0:2 * E].rearrange("p (q e) -> p q e", q=2),
                                  base[:, :].unsqueeze(1).to_broadcast([P, 2, E]), ALU.add)
                wait(dve, gsum_ready, d)
                dve.reciprocal(gate1[:, :], gsum[:, :])
                dve.drain()
                dve.tensor_tensor(base[:, :], TR[:, 2 * E:3 * E], base[:, :], ALU.add).then_inc(cs_read, 1)
                dve.tensor_tensor(posh[:, :, :], pos[:, :, :], hot[:, :, :], ALU.mult)
                dve.drain()
                dve.reduce_sum(pos1[:, :], posh[:, :, :], AX.X)
                dve.drain()
                dve.tensor_scalar(okf[:, :], pos1[:, :], float(CAP), None, ALU.is_lt)
                dve.scalar_tensor_tensor(slotf[:, :], idx_f[:, :], float(CAP), pos1[:, :], ALU.mult, ALU.add)
                dve.drain()
                dve.tensor_scalar(far[:, :], okf[:, :], -float(4 * NSLOT), float(4 * NSLOT), ALU.mult, ALU.add)
                dve.tensor_copy(xrow[:, :, GATE], gate1[:, :])
                dve.tensor_copy(xrow[:, :, TOKEN], left[:, :])
                dve.drain()
                if exists(back(d)):
                    dve.wait_ge(scat, nth(back(d), 32, 31))
                dve.tensor_tensor(slot_u[:, :], slotf[:, :], far[:, :], ALU.add).then_inc(slot_ready, 1)
                dve.tensor_scalar(left[:, :], left[:, :], -float(WIN), None, ALU.add)

            def step(s, par):
                a, c, d, f = stages(s)
                nxt = back(s, -1)
                first = a and (nxt[0] is not None or nxt[1] < NW)
                for k in range(UNITS):
                    if c and k == AT["split_g"]:
                        split_global_maxima(c)
                    for j in range(4):
                        if a and k == AT[f"p{j}"] + 1:
                            mid_part(j, a)
                    if f and k == AT["top"]:
                        route_top(f)
                    for q in range(2):
                        if d and k == AT[f"n_g{q}"]:
                            normalise(1, q, d)
                        if c and k == AT[f"n_l{q}"]:
                            normalise(0, q, c)
                    if first and k == AT["norm0"]:
                        first_stats(nxt, 1 - par)
                    if first and k == AT["norm0"] + 1:
                        first_norm(nxt, 1 - par)
                    if f and k == AT["cs"]:
                        route_slot(f)
                    if d and k == AT["op"]:
                        wait(dve, o_full, d)
                        wait(dve, y_ready, back(d))
                        dve.tensor_tensor(fbuf[:, :, :], TR[:, :].rearrange("p (q f) -> p q f", q=2),
                                          bias_row[:, :].unsqueeze(1).to_broadcast([P, 2, D]), ALU.add).then_inc(f_ready, 1)
                        dve.drain()
                        stats(1, fbuf, d)
                    if a:
                        for u in S1_AT.get(k, ()):
                            maximum(u, a)
                    if d and k == AT["stats_y"]:
                        wait(dve, y_ready, d)
                        stats(2, ybuf, d)
                    if d and k == AT["stats_x1"]:
                        wait(dve, x1_ready, d)
                        stats(3, x1, d)
                    if d and k == AT["xn2"]:
                        wait(dve, x2T_full, back(d))
                        wait(dve, o_norm, back(d))
                        norm(3, xn2, x1, xn2_ready, d)
                        dve.tensor_copy(xrow[:, :, MEAN], mv[:, 3, :, 0])
                        dve.tensor_copy(xrow[:, :, RSTD], rstd[:, 3, :])
                    if d and k == AT["stats_xn2"]:
                        dve.drain()
                        stats(4, xn2, d)

            steps(dve, step)

            def norms(e):
                r = e[1] % RING
                dve.wait_ge(er_in[r], ering(e, RING, 16 * NCH))
                if eexists(back(e, RING)):
                    dve.wait_ge(oe_out[r], ering(back(e, RING), RING, 16 * NCH))
                for lo, n, m in PIECES:
                    dve.tensor_scalar(idx_e[0:m, r, lo:lo + n], erows[0:m, r, lo:lo + n, TOKEN], -1.0, float(T), ALU.mult, ALU.add)
                for n, (lo, m) in enumerate(CHUNKS):
                    last = dve.tensor_scalar(zb[0:m, r, n, :], erows[0:m, r, n, 0:D], erows[0:m, r, n, MEAN:MEAN + 1],
                                             erows[0:m, r, n, RSTD:RSTD + 1], ALU.subtract, ALU.mult)
                last.then_inc(xe_ready, 1)

            def expert(e):
                ahead, last, old = back(e, -2), back(e), back(e, 2)
                if eexists(old):
                    r, b = old[1] % RING, old[1] % 2
                    dve.wait_ge(rs_ready, eth(old))
                    for n, (lo, m) in enumerate(CHUNKS):
                        done = dve.tensor_scalar(zb[0:m, r, n, :], zb[0:m, r, n, :], mv_e[0:m, b, n, 0:1], rs_e[0:m, b, n:n + 1],
                                                 ALU.subtract, ALU.mult)
                    done.then_inc(ne_ready, 1)
                if eexists(e):
                    for m in range(2):
                        dve.wait_ge(sg_ready, eth(e, 2, m))
                        dve.tensor_tensor(hT[:, e[1] % 2, m, :], banks[3 + 2 * m][:, 0:CAP], sg[:, m, :], ALU.mult).then_inc(h_ready, 1)
                if eexists(ahead):
                    norms(ahead)
                if eexists(last):
                    r, b = last[1] % RING, last[1] % 2
                    dve.wait_ge(ye_full, eth(last))
                    for n, (lo, m) in enumerate(CHUNKS):
                        done = dve.scalar_tensor_tensor(zb[0:m, r, n, :], banks[6 + n // 2][0:m, n % 2 * D:(n % 2 + 1) * D],
                                                        erows[0:m, r, n, GATE:GATE + 1], zb[0:m, r, n, :], ALU.mult, ALU.add)
                    done.then_inc(ze_ready, 1)
                    dve.drain()
                    for n, (lo, m) in enumerate(CHUNKS):
                        dve.bn_stats(bst_e[0:m, n, :], zb[0:m, r, n, :])
                    dve.drain()
                    for n, (lo, m) in enumerate(CHUNKS):
                        dve.bn_aggr(mv_e[0:m, b, n, :], bst_e[0:m, n, :])
                    dve.drain()
                    dve.tensor_scalar(ve_e[:, b, :], mv_e[:, b, :, 1], EPS, None, ALU.add).then_inc(ve_ready, 1)

            norms((None, 0))
            norms((None, 1))
            expert_turns(dve, expert, tail=2)

        @block.tensor
        def _(pe):
            n = 0
            for b in range(2):
                for c in range(2):
                    if c == 0:
                        pe.wait_ge(w_in[b], 32)
                    for half, (lo, width) in enumerate(((0, 512), (512, 256))):
                        for kc in range(2):
                            last = pe.matmul(banks[n + half][:, 0:width], pT[:, b, kc, c * P:(c + 1) * P],
                                             winT[:, b, kc, lo:lo + width], start=(kc == 0), stop=(kc == 1))
                        last.then_inc(w_fold, 1)
                    n += 2
            pe.wait_ge(w_fold_out, 4)
            pe.wait_ge(wo_ready, 1)
            for c in range(4):
                last = pe.matmul(TR[:, 0:D], bvb[:, c, :], wo[:, c, :], start=(c == 0), stop=(c == 3))
            last.then_inc(bias_ps, 1)
            pe.wait_ge(const_pool, 1)
            pe.wait_ge(w_fold_out, 4)
            pe.wait_ge(const_dve, 2)

            def scores(u, c, par):
                if u == 0:
                    for j in (0, 1):
                        pe.wait_ge(spread[j], nth(c, 96, 95))
                    pe.wait_ge(m_in[0], nth(c, 16, 15))
                if u == LU:
                    for j in (2, 3):
                        pe.wait_ge(spread[j], nth(c, 96, 95))
                    pe.wait_ge(m_in[1], nth(c, 16, 15))
                if u >= 2:
                    wait(pe, p_ready, c, UNITS, u - 2)
                else:
                    wait(pe, p_ready, back(c), UNITS, UNITS - 2 + u)
                bank = S2[u % 2]
                if u < LU:
                    pe.matmul(bank[:, :], identb[:, :], tri[:, :].unsqueeze(1).to_broadcast([P, 4, P]), start=True, stop=False)
                    for h2 in range(2):
                        for j in range(2):
                            h = 2 * u + h2
                            last = pe.matmul(bank[:, (2 * h2 + j) * P:(2 * h2 + j + 1) * P], k_stack(par, 0, h, j * P, P),
                                             q_stack(par, 0, h, j * P, P), start=False, stop=(h2 == 1 and j == 1))
                else:
                    diagonal = bank[:, :].rearrange("p (a n) -> p a n", n=P)[:, 0:4:3, :]
                    pe.matmul(diagonal, identb[:, :], tri[:, :].unsqueeze(1).to_broadcast([P, 2, P]), start=True, stop=False)
                    for kb in range(2):
                        for qb in range(2):
                            last = pe.matmul(bank[:, (2 * kb + qb) * P:(2 * kb + qb + 1) * P],
                                             k_stack(par, 1, u - LU, kb * P, P, BROW), q_stack(par, 1, u - LU, qb * P, P, BROW),
                                             start=False, stop=(kb == 1 and qb == 1))
                last.then_inc(s2_full, 1)

            def values(g, c, par):
                wait(pe, ot_ready, c if g else back(c), GROUPS, (g - 1) % GROUPS)
                if g < 4:
                    wait(pe, p_ready, c, UNITS, 2 * g + 1)
                    for j in range(2):
                        for h4 in range(4):
                            last = pe.matmul(PV[32 * h4:32 * h4 + 32, j * P:(j + 1) * P], v_pad[:, par, j, 0, 4 * g + h4, :],
                                             pt[:, (2 * g + h4 // 2) % 8, (2 * (h4 % 2) + j) * P:(2 * (h4 % 2) + j + 1) * P],
                                             start=True, stop=True)
                else:
                    u0 = LU + 4 * (g - 4)
                    wait(pe, p_ready, c, UNITS, u0 + 3)
                    for kb in range(2):
                        for h4 in range(4):
                            last = pe.matmul(PV[32 * h4:32 * h4 + 32, 0:WIN], v_pad[:, par, kb, 1, 4 * (g - 4) + h4, :],
                                             pt[:, (u0 + h4) % 8, kb * WIN:(kb + 1) * WIN], start=(kb == 0), stop=(kb == 1))
                last.then_inc(pv_full, 1)

            def project(j, a, s, par):
                if j:
                    wait_read(pe, PJ_USES, f"p{j}", s, 2)
                bank, b, qk = pj_bank(f"p{j}"), j // 2, j % 2
                for t in range(2):
                    for c in range(2):
                        last = pe.matmul(bank[:, t * WIN:(t + 1) * WIN], weff[:, b, c, qk * D + t * P:qk * D + (t + 1) * P],
                                         xnT[:, c, :], start=(c == 0), stop=(c == 1))
                last.then_inc(pj_full, 1)

            def project_v(q, a, s, par):
                wait_read(pe, PJ_USES, f"v{q}", s, 2)
                for c in range(2):
                    last = pe.matmul(pj_bank(f"v{q}")[:, :], xnT[:, c, q * P:(q + 1) * P], weff[:, :, c, 2 * D:3 * D],
                                     start=(c == 0), stop=(c == 1))
                last.then_inc(v_full, 1)

            def row_scores(u, a, par):
                if u == 0:
                    for j in (0, 1):
                        pe.wait_ge(spread[j], nth(a, 96, 95))
                if u == LU:
                    for j in (2, 3):
                        pe.wait_ge(spread[j], nth(a, 96, 95))
                if u >= 4:
                    wait(pe, s1_read, a, UNITS, u - 4)
                elif u >= 2:
                    wait(pe, s1_read, back(a), UNITS, UNITS - 4 + u)
                elif u == 0:
                    wait(pe, v_ready, a, 2, 1)
                bank = S1[u % 4]
                for n in range(2):
                    for j in range(2):
                        if u < LU:
                            last = pe.matmul(bank[:, (2 * n + j) * P:(2 * n + j + 1) * P], q_stack(par, 0, 2 * u + n, j * P, P, NPART),
                                             k_stack(par, 0, 2 * u + n, j * P, P, NPART), start=True, stop=True)
                        elif j == 0:
                            last = pe.matmul(bank[:, n * WIN:(n + 1) * WIN], q_stack(par, 1, u - LU, n * P, P, NPART),
                                             k_stack(par, 1, u - LU, 0, WIN, NPART), start=True, stop=True)
                last.then_inc(s1_full, 1)

            def four_transposes(src, sem_full):
                for n in range(4):
                    last = pe.transpose(TR[:, n * P:(n + 1) * P], src(n), ident[:, :])
                last.then_inc(sem_full, 1)

            def maxima_T(b, a, s):
                needs = [(mparts_ready[b], nth(a, 1))]
                before = read_before(TR_USES, ("mT_l", "mT_g")[b], s, 1)
                if before:
                    needs.append(before)
                needs = [(sem_, n if isinstance(n, int) else pe.to_reg(n)) for sem_, n in needs]
                pe.wait_ge(const_pool, 1)
                for sem_, n in needs:
                    pe.wait_ge(sem_, n)
                trb = TR[:, :].bitcast(bf16)
                for q in range(2):
                    last = pe.transpose(trb[0:48, q * P:(q + 1) * P], mparts[:, b, q, :, :].rearrange("p r h -> p (r h)"), identb[:, :])
                last.then_inc(mT_full[b], 1)

            def norm_T(b, q, w, s):
                wait_read(pe, TR_USES, f"n_{'lg'[b]}{q}", s, 1)
                wait(pe, ot_ready, w, GROUPS, 3 + 4 * b)
                four_transposes(lambda n: OT[:, b, n, q * P:(q + 1) * P], nrm_full[b])

            def out_T(b, w, s):
                wait_read(pe, TR_USES, f"oT_{'lg'[b]}", s, 1)
                wait(pe, on_ready[b], w, 2, 1)
                four_transposes(lambda n: On[:, b, n % 2, n // 2 * P:(n // 2 + 1) * P], onT_full[b])

            def step(s, par):
                a, c, d, f = stages(s)
                if s[0] is None and s[1] == 1:
                    pe.wait_ge(behind_in, 6 * 16)
                for k in range(UNITS):
                    if c:
                        scores(k, c, 1 - par)
                        if k in GROUP_AT:
                            values(GROUP_AT[k], c, 1 - par)
                    if f and k == AT["x2T"]:
                        wait_read(pe, TR_USES, "x2T", s, 1)
                        wait(pe, xn2_ready, f)
                        four_transposes(lambda n: xn2[:, n % 2, n // 2 * P:(n // 2 + 1) * P], x2T_full)
                    if d and k == LAST_GROUP_AT:
                        values(GROUPS - 1, d, par)
                    if a and k == AT["xnT"]:
                        wait(pe, s1_read, back(a), UNITS, UNITS - 3)
                        wait(pe, xn_ready, a)
                        bank = pj_bank("xnT")
                        for n in range(4):
                            last = pe.transpose(bank[:, n * P:(n + 1) * P], xn[:, n % 2, n // 2 * P:(n // 2 + 1) * P], ident[:, :])
                        last.then_inc(xnT_full, 1)
                    if a and k == AT["p0"]:
                        wait(pe, xnT_ready, a)
                    for j in range(4):
                        if a and k == AT[f"p{j}"]:
                            project(j, a, s, par)
                    for q in range(2):
                        if a and k == AT[f"v{q}"]:
                            project_v(q, a, s, par)
                    if f and k == AT["lg"]:
                        wait_read(pe, TR_USES, "lg", s, 1)
                        wait(pe, x2T_ready, f)
                        for q in range(2):
                            for n in range(2):
                                last = pe.matmul(TR[:, q * E:(q + 1) * E], xn2T[:, n, q * P:(q + 1) * P], wr[:, n, :],
                                                 start=(n == 0), stop=(n == 1))
                        last.then_inc(lg_full, 1)
                    for q in range(2):
                        if d and k == AT[f"n_g{q}"]:
                            norm_T(1, q, d, s)
                        if c and k == AT[f"n_l{q}"]:
                            norm_T(0, q, c, s)
                    if c and k == AT["mT_g"]:
                        maxima_T(1, c, s)
                    if d and k == AT["oT_g"]:
                        out_T(1, d, s)
                    if f and k == AT["cs"]:
                        wait_read(pe, TR_USES, "cs", s, 1)
                        wait(pe, hot_ready, f)
                        pe.matmul(TR[:, 0:E], earlier[:, :], hot[:, 0, :], start=True, stop=True)
                        pe.matmul(TR[:, E:2 * E], earlier[:, :], hot[:, 1, :], start=True, stop=False)
                        pe.matmul(TR[:, E:2 * E], onesb[:, :], hot[:, 0, :], start=False, stop=True)
                        pe.matmul(TR[:, 2 * E:3 * E], onesb[:, :], hot[:, 0, :], start=True, stop=False)
                        pe.matmul(TR[:, 2 * E:3 * E], onesb[:, :], hot[:, 1, :], start=False, stop=True).then_inc(cs_full, 1)
                    if d and k == AT["op"]:
                        wait_read(pe, TR_USES, "op", s, 1)
                        wait(pe, onT_ready[0], d)
                        wait(pe, onT_ready[1], d)
                        for q in range(2):
                            for n in range(4):
                                last = pe.matmul(TR[:, q * D:(q + 1) * D], OnT[:, n // 2, n % 2, q * P:(q + 1) * P], wo[:, n, :],
                                                 start=(n == 0), stop=(n == 3))
                        last.then_inc(o_full, 1)
                    if a and k == AT["mT_l"]:
                        maxima_T(0, a, s)
                    if c and k == AT["oT_l"]:
                        out_T(0, c, s)
                    if a:
                        for u in S1_AT.get(k, ()):
                            row_scores(u, a, par)

            steps(pe, step)

            def transposes(e):
                if eexists(back(e)):
                    pe.wait_ge(eT_ready, eth(back(e)))
                pe.wait_ge(xe_ready, eth(e))
                for c in range(2):
                    for n, (lo, m) in enumerate(CHUNKS):
                        last = pe.transpose(banks[c][:, lo:lo + m], zb[0:m, e[1] % RING, n, c * P:(c + 1) * P], ident[0:m, 0:m])
                last.then_inc(eT_full, 1)

            def gate_up(e):
                pe.wait_ge(gu_in[e[1] % 3], ering(e, 3, 32))
                pe.wait_ge(eT_ready, eth(e))
                for m in range(2):
                    if eexists(back(e)):
                        pe.wait_ge(h_ready, eth(back(e), 2, m))
                    for n in range(2):
                        for c in range(2):
                            last = pe.matmul(banks[2 + 2 * m + n][:, 0:CAP], ew[:, e[1] % 3, n, c, m * P:(m + 1) * P], eT[:, e[1] % 2, c, :],
                                             start=(c == 0), stop=(c == 1))
                    last.then_inc(gu_full, 1)

            def down(e):
                if eexists(back(e)):
                    pe.wait_ge(ze_ready, eth(back(e)))
                pe.wait_ge(down_in[e[1] % 3], ering(e, 3, 16))
                pe.wait_ge(h_ready, eth(e, 2, 1))
                for n, (lo, m) in enumerate(CHUNKS):
                    for c in range(2):
                        last = pe.matmul(banks[6 + n // 2][0:m, n % 2 * D:(n % 2 + 1) * D], hT[:, e[1] % 2, c, lo:lo + m],
                                         ew[:, e[1] % 3, 2, c, :], start=(c == 0), stop=(c == 1))
                last.then_inc(ye_full, 1)

            def expert(e):
                if eexists(e):
                    gate_up(e)
                if eexists(back(e, -1)):
                    transposes(back(e, -1))
                if eexists(back(e)):
                    down(back(e))

            pe.wait_ge(cs_read, NW)
            transposes((None, 0))
            expert_turns(pe, expert, tail=1)


def kernel(**inputs):
    import numpy as np
    import concourse.bacc as bacc
    from concourse.bass_utils import run_bass_kernel_spmd

    arrays = layouts(inputs)
    shape = arrays["x"].shape
    nc = bacc.Bacc("TRN2", target_bir_lowering=False, num_devices=1)
    args = {}
    for name, a in arrays.items():
        args[name] = nc.dram_tensor(name, a.shape, mybir.dt.from_np(a.dtype), kind="ExternalInput").ap()
    args["out"] = nc.dram_tensor("out", shape, mybir.dt.float32, kind="ExternalOutput").ap()
    attention_moe_program(nc, shape[0] * shape[1], **args)
    r = run_bass_kernel_spmd(nc, [arrays], core_ids=[0])
    return r.results[0]["out"]


def layouts(inputs):
    import numpy as np
    a = {n.split("_", 2)[2]: np.ascontiguousarray(v) for n, v in inputs.items()}
    out = {"x": a["x"]}
    for b, name in (("l", "local"), ("g", "global")):
        bias = a[f"b{b}_in"]
        out[f"pT_{b}"] = np.ascontiguousarray(a[f"proj_{name}"].T)
        out[f"winT_{b}"] = np.ascontiguousarray(a[f"W{b}_in"].T)
        out[f"woT_{b}"] = np.ascontiguousarray(a[f"W{b}_out"].T)
        out[f"bqk_{b}"] = np.ascontiguousarray(bias[:512].reshape(2, 2, 8, 16).transpose(3, 2, 0, 1).reshape(128, 4))
        out[f"bv_{b}"] = np.ascontiguousarray(bias[512:].reshape(2, 128).T)
        out[f"bo_{b}"] = a[f"b{b}_out"]
    out["fusion_w"] = a["fusion_w"]
    out["gamma"] = a["ln_gamma"]
    out["beta"] = a["ln_beta"]
    for n in ("w_router", "w_gate", "w_up", "w_down"):
        out[n] = a[n]
    return out
```
